# Optimizing a Trainium2 kernel written in Bass

```python
import numpy as np
import jax
import jax.numpy as jnp

def _softmax(x, axis=-1):
    return jax.nn.softmax(x, axis=axis)

def _gelu(x):
    return jax.nn.gelu(x, approximate=True)

def _silu(x):
    return jax.nn.silu(x)

def _sigmoid(x):
    return jax.nn.sigmoid(x)

def _layernorm(x, axis=-1, eps=1e-05):
    m = jnp.mean(x, axis=axis, keepdims=True)
    v = jnp.var(x, axis=axis, keepdims=True)
    return (x - m) / jnp.sqrt(v + eps)

def _scatter_add(tgt, idx, src, axis=0):
    return tgt.at[idx].add(src)

def _segment_sum(src, seg, n):
    return jax.ops.segment_sum(src, seg, n)
kernel_name = 'mk_flamingo_gated_d2_seqx_r4_401e59'

def setup_inputs(seed: int=0):
    np.random.seed(seed)
    _w = jnp.asarray

    def _rec_inputs():
        import jax
        import jax.numpy as jnp
        _rk = jax.random.key(seed)
        x = -0.0003929 + 0.9999 * jax.random.normal(jax.random.fold_in(_rk, 1), (8, 256, 256), jnp.float32)
        _lenS = 256 - jax.random.randint(jax.random.fold_in(_rk, 7), (8,), 0, max(1, 256 // 4) + 1, jnp.int32)
        _lenS2 = 256 - jax.random.randint(jax.random.fold_in(_rk, 8), (8,), 0, max(1, 256 // 4) + 1, jnp.int32)
        _ctx_1024P = jax.random.normal(jax.random.fold_in(_rk, 11), (8, 16, 256), jnp.float32)
        _ctx_1024c = jax.random.dirichlet(jax.random.fold_in(_rk, 511), 0.3 * jnp.ones((16,), jnp.float32), (8, 256))
        _ctx_1024t = jnp.einsum('bsk,bkd->bsd', _ctx_1024c, _ctx_1024P)
        _ctx_1024t = _ctx_1024t * jax.lax.rsqrt(jnp.mean(jnp.square(_ctx_1024t)) + 1e-12) * 0.953939
        ctx_1024 = 4.13588e-05 + 0.999923 * (_ctx_1024t + 0.3 * jax.random.normal(jax.random.fold_in(_rk, 611), (8, 256, 256), jnp.float32))
        _g = jax.random.normal(jax.random.fold_in(_rk, 9001), (2, 2), jnp.float32)
        _g = jnp.sign(_g) * jnp.maximum(jnp.abs(_g), 1.0) + (_g == 0) * 1.0
        g_xattn = _g[0]
        g_ffn = _g[1]
        return (x, ctx_1024, g_xattn, g_ffn)
    x, ctx_1024, g_xattn, g_ffn = _rec_inputs()

    def _L0_xattn_setup():
        import jax, jax.numpy as jnp
        import numpy as np
        H = 256
        B = 8
        L_CHAR = 512
        L_SUB = 256

        def _linear(x, W, b):
            return jnp.einsum('blh,oh->blo', x, W) + b

        def _interp_linear(x, out_len):
            L_in = x.shape[1]
            pos = (jnp.arange(out_len, dtype=x.dtype) + 0.5) * (L_in / out_len) - 0.5
            pos = jnp.clip(pos, 0.0, L_in - 1)
            lo = jnp.floor(pos).astype(jnp.int32)
            hi = jnp.minimum(lo + 1, L_in - 1)
            w = (pos - lo.astype(x.dtype))[None, :, None]
            return x[:, lo] * (1 - w) + x[:, hi] * w
        key = jax.random.key(seed)
        ks = jax.random.split(key, 18)
        s = 0.02
        inp = {'char_emb': jax.random.normal(ks[0], (B, L_CHAR, H), jnp.float32), 'subword_emb': jax.random.normal(ks[1], (B, L_SUB, H), jnp.float32)}
        names = ['Wq_c', 'Wk_s', 'Wv_s', 'Wq_s', 'Wk_c', 'Wv_c']
        for i, n in enumerate(names):
            inp[n] = jax.random.normal(ks[2 + 2 * i], (H, H), jnp.float32) * s
            inp['b' + n[1:]] = jax.random.normal(ks[3 + 2 * i], (H,), jnp.float32) * s
        inp['Wg'] = jax.random.normal(ks[14], (H, 2 * H), jnp.float32) * s
        inp['bg'] = jax.random.normal(ks[15], (H,), jnp.float32) * s
        return inp
    _L0_xattn_all = _L0_xattn_setup()
    _L0_xattn_in = {k: v for k, v in _L0_xattn_all.items() if k in ('Wq_c', 'bq_c', 'Wk_s', 'bk_s', 'Wv_s', 'bv_s', 'Wq_s', 'bq_s', 'Wk_c', 'bk_c', 'Wv_c', 'bv_c', 'Wg', 'bg')}
    del _L0_xattn_all

    def _L0_ffn_setup():
        import jax, jax.numpy as jnp
        import numpy as np
        B, S, D, E = (2, 512, 256, 8)
        key = jax.random.key(seed)
        ks = jax.random.split(key, 5)
        x = jax.random.normal(ks[0], (B, S, D), dtype=jnp.float32)
        router_w = jax.random.normal(ks[1], (E, D), dtype=jnp.float32) * 0.02
        router_b = jnp.zeros((E,), dtype=jnp.float32)
        expert_w = jax.random.normal(ks[2], (E, D, D), dtype=jnp.float32) * 0.02
        expert_b = jnp.zeros((E, D), dtype=jnp.float32)
        return {'x': x, 'router_w': router_w, 'router_b': router_b, 'expert_w': expert_w, 'expert_b': expert_b}
    _L0_ffn_all = _L0_ffn_setup()
    _L0_ffn_in = {k: v for k, v in _L0_ffn_all.items() if k in ('router_w', 'router_b', 'expert_w', 'expert_b')}
    del _L0_ffn_all

    def _L1_xattn_setup():
        import jax, jax.numpy as jnp
        import numpy as np
        D_MODEL = 256
        NUM_HEADS = 16
        HEAD_DIM = D_MODEL // NUM_HEADS
        MAX_SEQ = 128

        def rope_tables(seq_len, dim):
            inv_freq = 1.0 / 10000.0 ** (jnp.arange(0, dim, 2, dtype=jnp.float32) / dim)
            t = jnp.arange(seq_len, dtype=jnp.float32)
            freqs = jnp.einsum('i,j->ij', t, inv_freq)
            emb = jnp.concatenate([freqs, freqs], axis=-1)
            return (jnp.cos(emb), jnp.sin(emb))

        def rotate_half(x):
            x1, x2 = jnp.split(x, 2, axis=-1)
            return jnp.concatenate([-x2, x1], axis=-1)
        key = jax.random.key(seed)
        ks = jax.random.split(key, 12)
        B, S, D = (16, 128, D_MODEL)
        s = 1.0 / np.sqrt(D)
        inp = {'query': jax.random.normal(ks[0], (B, S, D), jnp.float32), 'key': jax.random.normal(ks[1], (B, S, D), jnp.float32), 'value': jax.random.normal(ks[2], (B, S, D), jnp.float32), 'Wq': jax.random.normal(ks[3], (D, D), jnp.float32) * s, 'bq': jnp.zeros((D,), jnp.float32), 'Wk': jax.random.normal(ks[4], (D, D), jnp.float32) * s, 'bk': jnp.zeros((D,), jnp.float32), 'Wv': jax.random.normal(ks[5], (D, D), jnp.float32) * s, 'bv': jnp.zeros((D,), jnp.float32), 'Wo': jax.random.normal(ks[6], (D, D), jnp.float32) * s, 'bo': jnp.zeros((D,), jnp.float32)}
        return inp
    _L1_xattn_all = _L1_xattn_setup()
    _L1_xattn_in = {k: v for k, v in _L1_xattn_all.items() if k in ('Wq', 'bq', 'Wk', 'bk', 'Wv', 'bv', 'Wo', 'bo')}
    del _L1_xattn_all

    def _L1_ffn_setup():
        import jax, jax.numpy as jnp
        import numpy as np
        E = 8
        TOP_K = 2
        H = 256
        I = 128
        B, S = (2, 512)

        def _moe_forward(hidden_states, w_gate, w_fc, w_proj):
            b, s, h = hidden_states.shape
            x = hidden_states.reshape(-1, h)
            T = x.shape[0]
            router_logits = x @ w_gate.T
            topk_vals, topk_idx = jax.lax.top_k(router_logits, TOP_K)
            router_weights = jax.nn.softmax(topk_vals.astype(jnp.float32), axis=-1).astype(x.dtype)
            gates = jnp.zeros((T, E), x.dtype).at[jnp.arange(T)[:, None], topk_idx].add(router_weights)
            hmid = jax.nn.gelu(jnp.einsum('th,eih->tei', x, w_fc), approximate=False)
            y = jnp.einsum('tei,ehi->teh', hmid, w_proj)
            out = jnp.einsum('teh,te->th', y, gates)
            return out.reshape(b, s, h)
        key = jax.random.key(seed)
        k0, k1, k2, k3 = jax.random.split(key, 4)
        std = 0.02
        return {'hidden_states': jax.random.normal(k0, (B, S, H), dtype=jnp.float32), 'w_gate': jax.random.normal(k1, (E, H), dtype=jnp.float32) * std, 'w_fc': jax.random.normal(k2, (E, I, H), dtype=jnp.float32) * std, 'w_proj': jax.random.normal(k3, (E, H, I), dtype=jnp.float32) * (std / np.sqrt(48.0))}
    _L1_ffn_all = _L1_ffn_setup()
    _L1_ffn_in = {k: v for k, v in _L1_ffn_all.items() if k in ('w_gate', 'w_fc', 'w_proj')}
    del _L1_ffn_all
    return {'x': x, 'ctx_1024': ctx_1024, 'g_xattn': g_xattn, 'g_ffn': g_ffn, 'L0_xattn_Wq_c': _L0_xattn_in['Wq_c'], 'L0_xattn_bq_c': _L0_xattn_in['bq_c'], 'L0_xattn_Wk_s': _L0_xattn_in['Wk_s'], 'L0_xattn_bk_s': _L0_xattn_in['bk_s'], 'L0_xattn_Wv_s': _L0_xattn_in['Wv_s'], 'L0_xattn_bv_s': _L0_xattn_in['bv_s'], 'L0_xattn_Wq_s': _L0_xattn_in['Wq_s'], 'L0_xattn_bq_s': _L0_xattn_in['bq_s'], 'L0_xattn_Wk_c': _L0_xattn_in['Wk_c'], 'L0_xattn_bk_c': _L0_xattn_in['bk_c'], 'L0_xattn_Wv_c': _L0_xattn_in['Wv_c'], 'L0_xattn_bv_c': _L0_xattn_in['bv_c'], 'L0_xattn_Wg': _L0_xattn_in['Wg'], 'L0_xattn_bg': _L0_xattn_in['bg'], 'L0_ffn_router_w': _L0_ffn_in['router_w'], 'L0_ffn_router_b': _L0_ffn_in['router_b'], 'L0_ffn_expert_w': _L0_ffn_in['expert_w'], 'L0_ffn_expert_b': _L0_ffn_in['expert_b'], 'L1_xattn_Wq': _L1_xattn_in['Wq'], 'L1_xattn_bq': _L1_xattn_in['bq'], 'L1_xattn_Wk': _L1_xattn_in['Wk'], 'L1_xattn_bk': _L1_xattn_in['bk'], 'L1_xattn_Wv': _L1_xattn_in['Wv'], 'L1_xattn_bv': _L1_xattn_in['bv'], 'L1_xattn_Wo': _L1_xattn_in['Wo'], 'L1_xattn_bo': _L1_xattn_in['bo'], 'L1_ffn_w_gate': _L1_ffn_in['w_gate'], 'L1_ffn_w_fc': _L1_ffn_in['w_fc'], 'L1_ffn_w_proj': _L1_ffn_in['w_proj']}

def reference(x, ctx_1024, g_xattn, g_ffn, L0_xattn_Wq_c, L0_xattn_bq_c, L0_xattn_Wk_s, L0_xattn_bk_s, L0_xattn_Wv_s, L0_xattn_bv_s, L0_xattn_Wq_s, L0_xattn_bq_s, L0_xattn_Wk_c, L0_xattn_bk_c, L0_xattn_Wv_c, L0_xattn_bv_c, L0_xattn_Wg, L0_xattn_bg, L0_ffn_router_w, L0_ffn_router_b, L0_ffn_expert_w, L0_ffn_expert_b, L1_xattn_Wq, L1_xattn_bq, L1_xattn_Wk, L1_xattn_bk, L1_xattn_Wv, L1_xattn_bv, L1_xattn_Wo, L1_xattn_bo, L1_ffn_w_gate, L1_ffn_w_fc, L1_ffn_w_proj):
    import jax
    import jax.numpy as jnp

    def _L0_xattn_ref(char_emb, subword_emb, Wq_c, bq_c, Wk_s, bk_s, Wv_s, bv_s, Wq_s, bq_s, Wk_c, bk_c, Wv_c, bv_c, Wg, bg):
        import jax, jax.numpy as jnp
        import numpy as np
        H = 256
        B = 8
        L_CHAR = 512
        L_SUB = 256

        def _linear(x, W, b):
            return jnp.einsum('blh,oh->blo', x, W) + b

        def _interp_linear(x, out_len):
            L_in = x.shape[1]
            pos = (jnp.arange(out_len, dtype=x.dtype) + 0.5) * (L_in / out_len) - 0.5
            pos = jnp.clip(pos, 0.0, L_in - 1)
            lo = jnp.floor(pos).astype(jnp.int32)
            hi = jnp.minimum(lo + 1, L_in - 1)
            w = (pos - lo.astype(x.dtype))[None, :, None]
            return x[:, lo] * (1 - w) + x[:, hi] * w
        h = char_emb.shape[-1]
        scale = 1.0 / jnp.sqrt(jnp.asarray(h, char_emb.dtype))
        Q_char = _linear(char_emb, Wq_c, bq_c)
        K_sub = _linear(subword_emb, Wk_s, bk_s)
        V_sub = _linear(subword_emb, Wv_s, bv_s)
        scores = jnp.einsum('bqh,bkh->bqk', Q_char, K_sub) * scale
        char2sub = jnp.einsum('bqk,bkh->bqh', jax.nn.softmax(scores, axis=-1), V_sub)
        Q_sub = _linear(subword_emb, Wq_s, bq_s)
        K_char = _linear(char_emb, Wk_c, bk_c)
        V_char = _linear(char_emb, Wv_c, bv_c)
        scores2 = jnp.einsum('bqh,bkh->bqk', Q_sub, K_char) * scale
        sub2char = jnp.einsum('bqk,bkh->bqh', jax.nn.softmax(scores2, axis=-1), V_char)
        L_char = char_emb.shape[1]
        if sub2char.shape[1] != L_char:
            sub2char = _interp_linear(sub2char, L_char)
        gate_in = jnp.concatenate([char2sub, sub2char], axis=-1)
        gate = jax.nn.sigmoid(jnp.einsum('blh,oh->blo', gate_in, Wg) + bg)
        return gate * char2sub + (1 - gate) * sub2char

    def _L0_ffn_ref(x, router_w, router_b, expert_w, expert_b):
        import jax, jax.numpy as jnp
        import numpy as np
        B, S, D, E = (2, 512, 256, 8)
        logits = jnp.einsum('bsd,ed->bse', x, router_w) + router_b
        probs = jax.nn.softmax(logits, axis=-1)
        weights = jnp.max(probs, axis=-1)
        top1 = jnp.argmax(probs, axis=-1)
        y_all = jnp.einsum('bsd,eod->bseo', x, expert_w) + expert_b
        y = jnp.take_along_axis(y_all, top1[:, :, None, None], axis=2)[:, :, 0, :]
        out = y * weights[:, :, None]
        return out

    def _L1_xattn_ref(query, key, value, Wq, bq, Wk, bk, Wv, bv, Wo, bo):
        import jax, jax.numpy as jnp
        import numpy as np
        D_MODEL = 256
        NUM_HEADS = 16
        HEAD_DIM = D_MODEL // NUM_HEADS
        MAX_SEQ = 128

        def rope_tables(seq_len, dim):
            inv_freq = 1.0 / 10000.0 ** (jnp.arange(0, dim, 2, dtype=jnp.float32) / dim)
            t = jnp.arange(seq_len, dtype=jnp.float32)
            freqs = jnp.einsum('i,j->ij', t, inv_freq)
            emb = jnp.concatenate([freqs, freqs], axis=-1)
            return (jnp.cos(emb), jnp.sin(emb))

        def rotate_half(x):
            x1, x2 = jnp.split(x, 2, axis=-1)
            return jnp.concatenate([-x2, x1], axis=-1)
        B, S, D = query.shape
        H, Hd = (NUM_HEADS, HEAD_DIM)
        scale = Hd ** (-0.5)

        def proj(x, W, b):
            y = jnp.einsum('bsd,ed->bse', x, W) + b
            return y.reshape(B, S, H, Hd).transpose(0, 2, 1, 3)
        q = proj(query, Wq, bq)
        k = proj(key, Wk, bk)
        v = proj(value, Wv, bv)
        cos, sin = rope_tables(S, Hd)
        cos = cos[None, None]
        sin = sin[None, None]
        q = q * cos + rotate_half(q) * sin
        k = k * cos + rotate_half(k) * sin
        attn = jnp.einsum('bhqd,bhkd->bhqk', q, k) * scale
        attn_w = jax.nn.softmax(attn, axis=-1)
        out = jnp.einsum('bhqk,bhkd->bhqd', attn_w, v)
        out = out.transpose(0, 2, 1, 3).reshape(B, S, D)
        out = jnp.einsum('bsd,ed->bse', out, Wo) + bo
        return out

    def _L1_ffn_ref(hidden_states, w_gate, w_fc, w_proj):
        import jax, jax.numpy as jnp
        import numpy as np
        E = 8
        TOP_K = 2
        H = 256
        I = 128
        B, S = (2, 512)

        def _moe_forward(hidden_states, w_gate, w_fc, w_proj):
            b, s, h = hidden_states.shape
            x = hidden_states.reshape(-1, h)
            T = x.shape[0]
            router_logits = x @ w_gate.T
            topk_vals, topk_idx = jax.lax.top_k(router_logits, TOP_K)
            router_weights = jax.nn.softmax(topk_vals.astype(jnp.float32), axis=-1).astype(x.dtype)
            gates = jnp.zeros((T, E), x.dtype).at[jnp.arange(T)[:, None], topk_idx].add(router_weights)
            hmid = jax.nn.gelu(jnp.einsum('th,eih->tei', x, w_fc), approximate=False)
            y = jnp.einsum('tei,ehi->teh', hmid, w_proj)
            out = jnp.einsum('teh,te->th', y, gates)
            return out.reshape(b, s, h)
        return _moe_forward(hidden_states, w_gate, w_proj=w_proj, w_fc=w_fc)
    x = x + jnp.tanh(g_xattn[0]) * _L0_xattn_ref(_layernorm(x, axis=-1), ctx_1024, L0_xattn_Wq_c, L0_xattn_bq_c, L0_xattn_Wk_s, L0_xattn_bk_s, L0_xattn_Wv_s, L0_xattn_bv_s, L0_xattn_Wq_s, L0_xattn_bq_s, L0_xattn_Wk_c, L0_xattn_bk_c, L0_xattn_Wv_c, L0_xattn_bv_c, L0_xattn_Wg, L0_xattn_bg)
    x = x + jnp.tanh(g_ffn[0]) * _L0_ffn_ref(_layernorm(x, axis=-1), L0_ffn_router_w, L0_ffn_router_b, L0_ffn_expert_w, L0_ffn_expert_b)
    x = x + jnp.tanh(g_xattn[1]) * _L1_xattn_ref(_layernorm(x, axis=-1), ctx_1024, ctx_1024, L1_xattn_Wq, L1_xattn_bq, L1_xattn_Wk, L1_xattn_bk, L1_xattn_Wv, L1_xattn_bv, L1_xattn_Wo, L1_xattn_bo)
    x = x + jnp.tanh(g_ffn[1]) * _L1_ffn_ref(_layernorm(x, axis=-1), L1_ffn_w_gate, L1_ffn_w_fc, L1_ffn_w_proj)
    return x

_drawn_inputs = setup_inputs


def setup_inputs(seed=0):
    import zlib

    import numpy as np

    out = dict(_drawn_inputs(seed))
    spreads = {'g_ffn': (-1.0, 0.6),
     'L0_ffn_router_b': (0.0, 0.353),
     'L0_ffn_expert_b': (0.0, 0.565),
     'L1_xattn_bq': (0.0, 0.543),
     'L1_xattn_bk': (0.0, 0.8),
     'L1_xattn_bv': (0.0, 0.1),
     'L1_xattn_bo': (0.0, 0.1)}
    factors = {'L0_xattn_Wq_c': 8.0,
     'L0_xattn_bq_c': 21.801,
     'L0_xattn_Wk_s': 8.0,
     'L0_xattn_bk_s': 64.0,
     'L0_xattn_bv_s': 7.29,
     'L0_xattn_Wq_s': 8.0,
     'L0_xattn_bq_s': 8.0,
     'L0_xattn_Wk_c': 8.0,
     'L0_xattn_bk_c': 64.0,
     'L0_xattn_Wv_c': 7.545,
     'L0_xattn_bv_c': 6.698,
     'L0_xattn_Wg': 8.0,
     'L0_xattn_bg': 8.0,
     'L1_ffn_w_gate': 8.0,
     'L1_ffn_w_fc': 8.0,
     'L1_ffn_w_proj': 8.0}
    for name, (base, spread) in spreads.items():
        noise = np.random.default_rng([zlib.crc32(name.encode()), seed]).standard_normal(out[name].shape)
        drawn = base * np.exp(spread * noise) if base else spread * noise
        out[name] = jnp.asarray(drawn.astype(out[name].dtype))
    for name, factor in factors.items():
        out[name] = (out[name] * factor).astype(out[name].dtype)
    return out
```

```python
from contextlib import ExitStack

import numpy as np

import concourse.bass as bass
from concourse import mybir

F32 = mybir.dt.float32
F32R = mybir.dt.float32r
BF16 = mybir.dt.bfloat16
U32 = mybir.dt.uint32
ALU = mybir.AluOpType
ACT = mybir.ActivationFunctionType
AX = mybir.AxisListType.X

NB = 8
S = 256
D = 256
E = 8
H = 16
EPS = 1e-5

MATS = ["qc", "kc", "qs", "ks", "vs", "vc", "g0", "g1"] + [f"e{i}" for i in range(8)] + \
       ["r"] + ["wq", "wk", "wv", "wo"] + [f"f{i}" for i in range(4)] + [f"p{i}" for i in range(4)]
MI = {n: i for i, n in enumerate(MATS)}
VEC = {n: 2 * i for i, n in enumerate(["qc", "kc", "qs", "ks", "vs", "vc", "g", "wq", "wk", "wv", "rb"])}


class Queue:

    def __init__(self, eng, sem, serial=False):
        self.eng, self.sem, self.n, self.seen, self.serial = eng, sem, 0, {}, serial

    def op(self, fn, waits=(), sig=True):
        if self.serial and self.n:
            waits = list(waits) + [(self.sem, self.n)]
        need = {}
        for sem, v in waits:
            if v > self.seen.get(id(sem), 0):
                self.seen[id(sem)] = v
                need[id(sem)] = (sem, v)
        for sem, v in need.values():
            self.eng.wait_ge(sem, v)
        i = fn(self.eng)
        if not sig:
            return []
        i.then_inc(self.sem, 1)
        self.n += 1
        return [(self.sem, self.n)]


def flamingo(nc, x_d, ctx_d, mats_d, vec_d, bo_d, g_d, eb_d, rope_d, iota_d, id_d, out_d):
    with ExitStack() as st:
        def sb(name, shape, dt=F32):
            return st.enter_context(nc.sbuf_tensor(name, shape, dt))

        nsem = [0]

        def sem():
            nsem[0] += 1
            return st.enter_context(nc.semaphore(f"s{nsem[0]}"))

        PE, AC, VE, SP = (Queue(e, sem()) for e in (nc.tensor, nc.scalar, nc.vector, nc.sync))
        PO = Queue(nc.gpsimd, sem(), serial=True)

        def dma(parts, waits=(), q=None):
            q = q or SP
            s = sem()
            for i, (o, a) in enumerate(parts):
                q.op(lambda e, o=o, a=a: e.dma_start(o, a).then_inc(s, 16), waits if i == 0 else (), sig=False)
            return [(s, 16 * len(parts))]

        T = {}

        def W(name, b):
            return T[name, b] if b >= 0 else []

        xall = sb("xall", [128, NB, 2, 256])
        vec = sb("vec", [128, 22])
        gb = sb("gb", [128, 4])
        tg = sb("tg", [128, 4])
        htg = sb("htg", [128, 4])
        hbg = sb("hbg", [128, 2])
        bo = sb("bo", [128, 256])
        rope = sb("rope", [128, 2, 256])
        iota = sb("iota", [128, 8])
        ident = sb("ident", [128, 128])
        nhalf = sb("nhalf", [128, 2])
        stage = sb("stage", [128, 4, 512])
        wr_h = sb("wr_h", [128, 512], F32R)
        wr_l = sb("wr_l", [128, 512], F32R)
        wA = [sb(f"wA{i}", [128, 8, 512], F32R) for i in range(2)]
        wB = [sb(f"wB{i}", [128, 8, 512], F32R) for i in range(2)]
        base = {}
        for i, n in enumerate(MATS):
            if n == "r":
                base[n] = (wr_h[:, :], wr_l[:, :])
            else:
                j = i if i < 16 else i - 17
                reg = wA if (i < 8 or 17 <= i < 21) else wB
                k = i if i < 8 else (i - 8 if i < 16 else (i - 17 if i < 21 else i - 21))
                base[n] = (reg[0][:, k, :], reg[1][:, k, :])
        xn = sb("xn", [128, 2, 256])
        stt = sb("stt", [128, 2, 6])
        mv = sb("mv", [128, 2, 2])
        ve = sb("ve", [128, 2])
        rstd = sb("rstd", [128, 2])
        xh = sb("xh", [128, 2, 256], F32R)
        xl = sb("xl", [128, 2, 256], F32R)
        lt = sb("lt", [128, 256])
        lg = sb("lg", [128, 2, 8])
        mx8 = sb("mx8", [128, 2, 8])
        ix8 = sb("ix8", [128, 2, 8], U32)
        ixf = sb("ixf", [128, 2, 8])
        oh1 = sb("oh1", [128, 2, 8])
        oh2 = sb("oh2", [128, 2, 8])
        rex = sb("rex", [128, 2, 8])
        rsm = sb("rsm", [128, 2, 4])
        gat = sb("gat", [128, 2, 2, 8])
        cx = sb("cx", [128, 2, 512])
        ch = sb("ch", [128, 2, 256], F32R)
        cl = sb("cl", [128, 2, 256], F32R)
        psum = st.enter_context(nc.psum_tensor("psum", [128, 8, 512], F32))
        bank_free = [[] for _ in range(8)]

        class Ring:
            def __init__(self, banks, width=1):
                self.banks, self.width, self.at = banks, width, 0

            def take(self):
                k = (self.at * self.width) % len(self.banks)
                self.at += 1
                bs = self.banks[k:k + self.width]
                waits = [t for b in bs for t in bank_free[b]]
                for b in bs:
                    bank_free[b] = None
                return bs, psum[:, bs[0]:bs[0] + self.width, :].rearrange("p a n -> p (a n)"), waits

        def release(bs, toks):
            for b in bs:
                bank_free[b] = list(toks)

        def hl(pair, f):
            return f(pair[0]), f(pair[1])

        def mm3(out, lhs, rhs, start, stop, waits=(), sig=False):
            seq = [(lhs[0], rhs[0]), (lhs[0], rhs[1]), (lhs[1], rhs[0])]
            tok = []
            for i, (a, m) in enumerate(seq):
                last = i == 2
                tok = PE.op(lambda e, a=a, m=m, i=i, last=last: e.matmul(out, a, m, start=start and i == 0, stop=stop and last),
                            waits if i == 0 else (), sig=sig and last)
            return tok

        ph1 = ExitStack()

        def s1(name, shape, dt=F32):
            return ph1.enter_context(nc.sbuf_tensor(name, shape, dt))

        pr = {n: (s1(n + "h", [128, 2, 256], F32R), s1(n + "l", [128, 2, 256], F32R)) for n in ["qc", "kc", "qs", "ks"] + [f"{v}{i}" for v in ("vs", "vc") for i in range(3)]}
        P1 = [s1(f"P1{i}", [128, 2, 256]) for i in range(2)]
        PT1 = [(s1(f"PT{i}h", [128, 2, 256], F32R), s1(f"PT{i}l", [128, 2, 256], F32R)) for i in range(2)]
        sm = [s1(f"sm{i}", [128, 8]) for i in range(2)]
        cf = [s1(f"cf{i}", [128, 2, 256]) for i in range(2)]
        cs = [(s1(f"cs{i}h", [128, 2, 256], F32R), s1(f"cs{i}l", [128, 2, 256], F32R)) for i in range(2)]
        gt = s1("gt", [128, 2, 256])
        dd = s1("dd", [128, 2, 256])
        uu = s1("uu", [128, 2, 256])
        mxn = s1("mxn", [128, 2, 256])
        x2h = s1("x2h", [128, 2, 256], F32R)
        x2l = s1("x2l", [128, 2, 256], F32R)
        ebh = s1("ebh", [128, 256], F32R)
        ebl = s1("ebl", [128, 256], F32R)
        gpad = s1("gpad", [128, 2, 128])
        gTh = s1("gTh", [128, 256], F32R)
        gTl = s1("gTl", [128, 256], F32R)

        c_vec = dma([(vec[:, :], vec_d)])
        c_id = dma([(ident[:, :], id_d)])
        c_g = dma([(gb[:, :], g_d)])
        tok_x = {}
        for b in range(NB):
            if b < 2:
                T["x", b] = dma([(xall[:, b, :, :], x_d[b])])

        def load_ctx(name, b, waits):
            T["cx", name, b] = dma([(cx[:, b % 2, :], ctx_d[b])], waits)

        PO.op(lambda e: e.memset(nhalf[:, :], -0.5))
        c_nh = PO.op(lambda e: e.memset(gpad[:, :, :], 0.0))
        c_tg = AC.op(lambda e: e.activation(tg[:, :], gb[:, :], ACT.Tanh), c_g)
        c_hbg = VE.op(lambda e: e.tensor_scalar(hbg[:, :], vec[:, VEC["g"]:VEC["g"] + 2], 0.5, None, ALU.mult), c_vec)

        load_ctx("A", 0, ())
        stage_free = [[] for _ in range(4)]
        wtok = {}
        nst = [0]

        def load_mat(n, waits=()):
            k = nst[0] % 4
            nst[0] += 1
            t = dma([(stage[:, k, :], mats_d[:, MI[n], :])], stage_free[k])
            h, l = base[n]
            a = AC.op(lambda e: e.activation(h, stage[:, k, :], ACT.Copy), t + list(waits))
            v = VE.op(lambda e: e.tensor_tensor(l, stage[:, k, :], h.bitcast(F32), ALU.subtract), a + t)
            stage_free[k] = v
            wtok[n] = v

        ln_free = {"xn": [], "x": []}
        ring = Ring(list(range(8)))
        G = [ring]

        def layer_norm(b, x_tok):
            s = []
            for t in range(2):
                s += VE.op(lambda e, t=t: e.bn_stats(stt[:, t, :], xall[:, b, t, :]), x_tok)
            a = []
            for t in range(2):
                a += VE.op(lambda e, t=t: e.bn_aggr(mv[:, t, :], stt[:, t, :]), s)
            p1 = PO.op(lambda e: e.tensor_scalar(ve[:, :], mv[:, :, 1], EPS, None, ALU.add), a + c_nh)
            p2 = PO.op(lambda e: e.tensor_tensor(rstd[:, :], ve[:, :], nhalf[:, :], ALU.pow), p1)
            n = []
            for t in range(2):
                n += VE.op(lambda e, t=t: e.tensor_scalar(xn[:, t, :], xall[:, b, t, :], mv[:, t, 0:1],
                                                          rstd[:, t:t + 1], ALU.subtract, ALU.mult), p2 + ln_free["xn"])
            return n

        def transpose4(src, toks):
            bs, ps, w = G[0].take()
            for k in range(2):
                for t in range(2):
                    tok = PE.op(lambda e, k=k, t=t: e.transpose(ps[:, k * 256 + t * 128:k * 256 + t * 128 + 128],
                                                               src[:, t, k * 128:(k + 1) * 128], ident[:, :]),
                                w + list(toks) + c_id, sig=(k == 1 and t == 1))
                    w = []
            return bs, ps, tok

        def split(bs, ps, tok, h, l, free, bias=None):
            hf, lf = h.rearrange("p a n -> p (a n)"), l.rearrange("p a n -> p (a n)")
            if bias is None:
                a = AC.op(lambda e: e.activation(hf, ps, ACT.Copy), tok + list(free))
                v = VE.op(lambda e: e.tensor_tensor(lf, ps, hf.bitcast(F32), ALU.subtract), a)
            else:
                for k in range(2):
                    a = AC.op(lambda e, k=k: e.activation(h[:, k, :], ps[:, k * 256:(k + 1) * 256], ACT.Identity,
                                                          bias=bias[:, k:k + 1]), tok + list(free) + c_vec)
                for k in range(2):
                    v = VE.op(lambda e, k=k: e.scalar_tensor_tensor(
                        out=l[:, k, :], in0=ps[:, k * 256:(k + 1) * 256], scalar=bias[:, k:k + 1],
                        in1=h[:, k, :].bitcast(F32), op0=ALU.add, op1=ALU.subtract), a)
            release(bs, v)
            return v

        def norm_T(b, x_tok, hh, ll, used):
            n = layer_norm(b, x_tok)
            bs, ps, tok = transpose4(xn, n)
            ln_free["xn"] = tok
            return split(bs, ps, tok, hh, ll, used)

        def proj_T(w, act, waits):
            bs, ps, pw = G[0].take()
            pw = pw + list(waits) + wtok[w]
            for o in range(2):
                for k in range(2):
                    tok = mm3(ps[:, o * 256:(o + 1) * 256], hl(base[w], lambda m: m[:, k * 256 + o * 128:k * 256 + o * 128 + 128]),
                              hl(act, lambda a: a[:, k, :]), k == 0, k == 1, pw, sig=(o == 1 and k == 1))
                    pw = []
            return bs, ps, tok

        def proj_N(w, act, waits):
            bs, ps, pw = G[0].take()
            pw = pw + list(waits) + wtok[w]
            for t in range(2):
                for k in range(2):
                    tok = mm3(ps[:, t * 256:(t + 1) * 256], hl(act, lambda a: a[:, k, t * 128:(t + 1) * 128]),
                              hl(base[w], lambda m: m[:, k * 256:(k + 1) * 256]), k == 0, k == 1, pw, sig=(t == 1 and k == 1))
                    pw = []
            return bs, ps, tok

        def router(b, half, act, waits, first):
            bs, ps, pw = G[0].take()
            pw = pw + list(waits) + wtok["r"]
            for k in range(2):
                tok = mm3(ps[:, 0:256], hl(base["r"], lambda m: m[:, half * 256 + k * 128:half * 256 + k * 128 + 128]),
                          hl(act, lambda a: a[:, k, :]), k == 0, k == 1, pw, sig=(k == 1))
                pw = []
            if first:
                a = AC.op(lambda e: e.activation(lt[0:8, :], ps[0:8, 0:256], ACT.Identity, bias=vec[0:8, VEC["rb"]:VEC["rb"] + 1]),
                          tok + W("lt", b - 1))
            else:
                a = AC.op(lambda e: e.activation(lt[0:8, :], ps[0:8, 0:256], ACT.Copy), tok + W("lt", b - 1))
            release(bs, a)
            bs, ps, pw = G[0].take()
            for t in range(2):
                tok = PE.op(lambda e, t=t: e.transpose(ps[:, t * 8:t * 8 + 8], lt[0:8, t * 128:(t + 1) * 128], ident[0:8, 0:8]),
                            pw + a, sig=(t == 1))
                pw = []
            T["lt", b] = tok
            v = VE.op(lambda e: e.tensor_copy(lg[:, :, :].rearrange("p a n -> p (a n)"), ps[:, 0:16]), tok)
            release(bs, v)
            m, i = [], []
            for t in range(2):
                m += VE.op(lambda e, t=t: e.max(mx8[:, t, :], lg[:, t, :]), v)
            for t in range(2):
                i += VE.op(lambda e, t=t: e.max_index(ix8[:, t, :], mx8[:, t, :], lg[:, t, :]), m)
            f = VE.op(lambda e: e.tensor_copy(ixf[:, :, :], ix8[:, :, :]), i + c_iota)
            o = []
            for t in range(2):
                o += VE.op(lambda e, t=t: e.tensor_scalar(oh1[:, t, :], iota[:, :], ixf[:, t, 0:1], None, ALU.is_equal), f)
                if not first:
                    o += VE.op(lambda e, t=t: e.tensor_scalar(oh2[:, t, :], iota[:, :], ixf[:, t, 1:2], None, ALU.is_equal), f)
            return m, o

        def A0(b):
            if b + 1 < NB:
                load_ctx("A", b + 1, W("ctxsplit", b - 1))
            if b + 2 < NB:
                T["x", b + 2] = dma([(xall[:, b + 2, :, :], x_d[b + 2])])
            f = W("projA", b - 1)
            a = AC.op(lambda e: e.activation(ch[:, :, :].rearrange("p a n -> p (a n)"), cx[:, b % 2, :], ACT.Copy), T["cx", "A", b] + f)
            T["ctxsplit", b] = VE.op(lambda e: e.tensor_tensor(cl[:, :, :].rearrange("p a n -> p (a n)"), cx[:, b % 2, :],
                                     ch[:, :, :].rearrange("p a n -> p (a n)").bitcast(F32), ALU.subtract), a + f)
            T["xA", b] = norm_T(b, T["x", b], xh, xl, f)

        def A1(b):
            C, X = (ch, cl), (xh, xl)
            toks = []
            for n, act, tr in [("qc", X, 1), ("ks", C, 1), ("qs", C, 1), ("kc", X, 1), ("vs", C, 0), ("vc", X, 0)]:
                bs, ps, tok = (proj_T if tr else proj_N)(n, act, T["xA", b] + T["ctxsplit", b])
                free = W("S0", b - 1) if n in ("qc", "ks") else W("S1", b - 1) if tr else W("PV" + str(int(n == "vc")), b - 3)
                T[n, b] = split(bs, ps, tok, *pr[n if tr else f"{n}{b % 3}"], free, bias=vec[:, VEC[n]:VEC[n] + 2] if tr else None)
            T["projA", b] = tok

        def A2(b):
            for i, (q, k) in enumerate([("qc", "ks"), ("qs", "kc")]):
                bs, ps, pw = G[0].take()
                pw = pw + T[q, b] + T[k, b]
                for t in range(2):
                    for kk in range(2):
                        tok = mm3(ps[:, t * 256:(t + 1) * 256], hl(pr[q], lambda m: m[:, kk, t * 128:(t + 1) * 128]),
                                  hl(pr[k], lambda m: m[:, kk, :]), kk == 0, kk == 1, pw, sig=(t == 1 and kk == 1))
                        pw = []
                T[f"S{i}", b] = tok
                s = sm[i]
                v = VE.op(lambda e: e.tensor_reduce(s[:, 0:2], ps.rearrange("p (a n) -> p a n", a=2), AX, ALU.max, negate=True), tok + W(f"P{i}", b - 1))
                v = VE.op(lambda e: e.tensor_scalar(s[:, 2:4], s[:, 0:2], 1.0 / 16, None, ALU.mult), v)
                for t in range(2):
                    a = AC.op(lambda e, t=t: e.activation(P1[i][:, t, :], ps[:, t * 256:(t + 1) * 256], ACT.Exp, bias=s[:, 2 + t:3 + t],
                                                     scale=1.0 / 16, accum_out=s[:, 4 + t:5 + t]), v + W(f"PTt{i}", b - 1))
                release(bs, a)
                v = VE.op(lambda e: e.reciprocal(s[:, 6:8], s[:, 4:6]), a)
                r = []
                for t in range(2):
                    r += VE.op(lambda e, t=t: e.tensor_scalar(P1[i][:, t, :], P1[i][:, t, :], s[:, 6 + t:7 + t], None, ALU.mult), v)
                T[f"P{i}", b] = r

        def A3(b):
            for i in range(2):
                bs, ps, tok = transpose4(P1[i], T[f"P{i}", b])
                T[f"PTt{i}", b] = tok
                T[f"PT{i}", b] = split(bs, ps, tok, *PT1[i], W(f"PV{i}", b - 1))

        def A4(b):
            for i, v_ in enumerate(["vs", "vc"]):
                bs, ps, pw = G[0].take()
                pw = pw + T[f"PT{i}", b] + T[v_, b]
                for o in range(2):
                    for k in range(2):
                        tok = mm3(ps[:, o * 256:(o + 1) * 256], hl(pr[f"{v_}{b % 3}"], lambda m: m[:, k, o * 128:(o + 1) * 128]),
                                  hl(PT1[i], lambda m: m[:, k, :]), k == 0, k == 1, pw, sig=(o == 1 and k == 1))
                        pw = []
                T[f"PV{i}", b] = tok
                bias = vec[:, VEC[v_]:VEC[v_] + 2]
                for k in range(2):
                    a = AC.op(lambda e, k=k: e.activation(cf[i][:, k, :], ps[:, k * 256:(k + 1) * 256], ACT.Identity, bias=bias[:, k:k + 1]),
                              tok + W("mix", b - 1))
                release(bs, a)
                v = VE.op(lambda e: e.tensor_copy(cs[i][0][:, :, :], cf[i][:, :, :]), a + W("gate", b - 1))
                T[f"cs{i}", b] = VE.op(lambda e: e.tensor_tensor(cs[i][1][:, :, :], cf[i][:, :, :], cs[i][0][:, :, :].bitcast(F32), ALU.subtract), v)

        def A5(b):
            bs, ps, pw = G[0].take()
            pw = pw + T["cs0", b] + T["cs1", b] + wtok["g0"] + wtok["g1"]
            for o in range(2):
                for k in range(4):
                    tok = mm3(ps[:, o * 256:(o + 1) * 256], hl(base[f"g{k // 2}"], lambda m: m[:, (k % 2) * 256 + o * 128:(k % 2) * 256 + o * 128 + 128]),
                              hl(cs[k // 2], lambda m: m[:, k % 2, :]), k == 0, k == 3, pw, sig=(o == 1 and k == 3))
                    pw = []
            T["gate", b] = tok
            for k in range(2):
                a = AC.op(lambda e, k=k: e.activation(gt[:, k, :], ps[:, k * 256:(k + 1) * 256], ACT.Tanh, bias=hbg[:, k:k + 1], scale=0.5),
                          tok + c_hbg + W("mix", b - 1))
            release(bs, a)
            p = PO.op(lambda e: e.tensor_tensor(dd[:, :, :], cf[0][:, :, :], cf[1][:, :, :], ALU.subtract), T["cs0", b] + T["cs1", b])
            v1 = VE.op(lambda e: e.tensor_tensor(uu[:, :, :], cf[0][:, :, :], cf[1][:, :, :], ALU.add), W("mix", b - 1))
            v = VE.op(lambda e: e.tensor_tensor(dd[:, :, :], dd[:, :, :], gt[:, :, :], ALU.mult), a + p)
            v = VE.op(lambda e: e.tensor_tensor(uu[:, :, :], uu[:, :, :], dd[:, :, :], ALU.add), v + v1)
            T["mix", b] = v
            bs, ps, pw = G[0].take()
            pw = pw + v
            for t in range(2):
                for k in range(2):
                    tok = PE.op(lambda e, t=t, k=k: e.transpose(ps[:, t * 256 + k * 128:t * 256 + k * 128 + 128], uu[:, k, t * 128:(t + 1) * 128],
                                                                ident[:, :]), pw, sig=(t == 1 and k == 1))
                    pw = []
            T["mix", b] = tok
            X = xall[:, b, :, :].rearrange("p a n -> p (a n)")
            v = VE.op(lambda e: e.scalar_tensor_tensor(out=X, in0=ps, scalar=htg[:, 0:1], in1=X, op0=ALU.mult, op1=ALU.add), tok + c_htg)
            release(bs, v)
            T["x1", b] = v

        def B0(b):
            T["xB", b] = norm_T(b, T["x1", b], x2h, x2l, W("exp", b - 1))
            m, o = router(b, 0, (x2h, x2l), T["xB", b], True)
            v = VE.op(lambda e: e.tensor_tensor(rex[:, :, :], lg[:, :, :], mx8[:, :, 0:1].broadcast_to([128, 2, 8]), ALU.subtract), m)
            a = AC.op(lambda e: e.activation(rex[:, :, :], rex[:, :, :], ACT.Exp), v)
            v = VE.op(lambda e: e.reduce_sum(rsm[:, :, 0], rex[:, :, :], axis=AX), a)
            v = VE.op(lambda e: e.reciprocal(rsm[:, :, 1], rsm[:, :, 0]), v)
            v = VE.op(lambda e: e.tensor_scalar(rsm[:, :, 2], rsm[:, :, 1], tg[:, 2:3], None, ALU.mult), v + c_tg)
            v = VE.op(lambda e: e.tensor_tensor(gat[:, b % 2, :, :], oh1[:, :, :], rsm[:, :, 2:3].broadcast_to([128, 2, 8]), ALU.mult), v + o + W("x2", b - 2))
            T["gat", b] = v
            v = VE.op(lambda e: e.tensor_copy(gpad[:, :, 0:8], gat[:, b % 2, :, :]), v + W("gTt", b - 1) + c_nh)
            bs, ps, pw = G[0].take()
            for t in range(2):
                tok = PE.op(lambda e, t=t: e.transpose(ps[:, t * 128:(t + 1) * 128], gpad[:, t, :], ident[:, :]), pw + v, sig=(t == 1))
                pw = []
            T["gTt", b] = tok
            a = AC.op(lambda e: e.activation(gTh[:, :], ps[:, 0:256], ACT.Copy), tok + W("bias", b - 1))
            v = VE.op(lambda e: e.tensor_tensor(gTl[:, :], ps[:, 0:256], gTh[:, :].bitcast(F32), ALU.subtract), a)
            release(bs, v)
            T["gT", b] = v

        def B1(b):
            bs, ps, pw = G[0].take()
            pw = pw + T["gT", b] + c_eb
            for t in range(2):
                tok = mm3(ps[:, t * 256:(t + 1) * 256], hl((gTh, gTl), lambda m: m[:, t * 128:(t + 1) * 128]), (ebh[:, :], ebl[:, :]), True, True, pw, sig=(t == 1))
                pw = []
            T["bias", b] = tok
            X = xall[:, b, :, :].rearrange("p a n -> p (a n)")
            v = VE.op(lambda e: e.tensor_tensor(X, ps, X, ALU.add), tok)
            release(bs, v)
            acc = [v, v]
            for x_ in range(8):
                bs, ps, tok = proj_N(f"e{x_}", (x2h, x2l), T["xB", b])
                for t in range(2):
                    acc[t] = VE.op(lambda e, t=t: e.scalar_tensor_tensor(
                        out=xall[:, b, t, :], in0=ps[:, t * 256:(t + 1) * 256], scalar=gat[:, b % 2, t, x_:x_ + 1],
                        in1=xall[:, b, t, :], op0=ALU.mult, op1=ALU.add), tok + acc[t] + T["gat", b])
                release(bs, acc[0] + acc[1])
            T["exp", b] = tok
            T["x2", b] = acc[0] + acc[1]

        for n in ["qc", "ks", "qs", "kc", "vs", "vc"]:
            load_mat(n)
        c_htg = VE.op(lambda e: e.tensor_scalar(htg[:, :], tg[:, :], 0.5, None, ALU.mult), c_tg)
        load_mat("g0")
        load_mat("g1")
        load_mat("r")
        ek = nst[0] % 4
        nst[0] += 1
        c_iota = dma([(iota[:, :], iota_d), (stage[:, ek, 0:256], eb_d), (bo[:, :], bo_d), (rope[:, :, :], rope_d)], stage_free[ek])
        t_ = AC.op(lambda e: e.activation(ebh[:, :], stage[:, ek, 0:256], ACT.Copy), c_iota)
        c_eb = VE.op(lambda e: e.tensor_tensor(ebl[:, :], stage[:, ek, 0:256], ebh[:, :].bitcast(F32), ALU.subtract), t_)
        stage_free[ek] = c_eb
        c_tbo = VE.op(lambda e: e.tensor_scalar(bo[:, :], bo[:, :], tg[:, 1:2], None, ALU.mult), c_iota + c_tg)
        for n in range(8):
            load_mat(f"e{n}")

        stages = [A0, A1, A2, A3, A4, A5, B0, B1]
        for step in range(NB + len(stages) - 1):
            for s in reversed(range(len(stages))):
                if 0 <= step - s < NB:
                    stages[s](step - s)
        ph1.close()
        endA = T["projA", NB - 1] + T["gate", NB - 1]
        endB = T["exp", NB - 1]
        end1 = T["x2", NB - 1] + endB + T["mix", NB - 1] + T["bias", NB - 1]

        qp = sb("qp", [128, 2, 2, 256])
        qr = sb("qr", [128, 2, 2, 256])
        qt = sb("qt", [128, 2, 2, 256])
        parts = sb("parts", [128, 2, 3, 2, 256], BF16)
        st_ = [sb(f"st{i}", [99, 2, H, 256], BF16) for i in range(2)]
        vv = [sb(f"vv{i}", [128, 2, H, 32]) for i in range(3)]
        mpad = sb("mpad", [128, 2, 128])
        mT = sb("mT", [16, 2, 256])
        mpt = sb("mpt", [16, 3, 256], BF16)
        PT = sb("PT", [128, 4, 2, 2, 256])
        OT = sb("OT", [128, 4, 256])
        rd = sb("rd", [128, 2, H])
        On = sb("On", [128, 2, 256])
        oT = (sb("oTh", [128, 2, 256], F32R), sb("oTl", [128, 2, 256], F32R))

        for n in ["wq", "wk", "wv", "wo"]:
            load_mat(n, endA)
        k2 = PO.op(lambda e: e.memset(mpad[:, :, :], 0.0), end1)
        for i in range(3):
            k2 = PO.op(lambda e, i=i: e.memset(vv[i][:, :, :, 16:32], 0.0), end1)
        for i in range(2):
            k2 = PO.op(lambda e, i=i: e.memset(st_[i][96:99, 1, :, :], 1.0), end1)
        for i in range(3):
            k2 = PO.op(lambda e, i=i: e.memset(vv[i][:, :, :, 16:17], 1.0), k2)
        for n in ["f0", "f1", "f2", "f3", "p0", "p1", "p2", "p3"]:
            load_mat(n, endB)
        gring, mring, ering = Ring([0, 1]), Ring([2, 3]), Ring([4, 5, 6, 7], 2)
        G[0] = gring

        def C0(b):
            if b == 0:
                load_ctx("C", 0, W("ctxsplit", NB - 1))
            if b + 1 < NB:
                load_ctx("C", b + 1, W("ctxsplitC", b - 1) if b else W("ctxsplit", NB - 1))
            f = W("projC", b - 1) if b else T["projA", NB - 1]
            a = AC.op(lambda e: e.activation(ch[:, :, :].rearrange("p a n -> p (a n)"), cx[:, b % 2, :], ACT.Copy), T["cx", "C", b] + f)
            T["ctxsplitC", b] = VE.op(lambda e: e.tensor_tensor(cl[:, :, :].rearrange("p a n -> p (a n)"), cx[:, b % 2, :],
                                      ch[:, :, :].rearrange("p a n -> p (a n)").bitcast(F32), ALU.subtract), a + f)
            T["xC", b] = norm_T(b, T["x2", b], xh, xl, f)

        def C1(b):
            C, X = (ch, cl), (xh, xl)
            for i, (n, act) in enumerate([("wq", X), ("wk", C)]):
                bs, ps, tok = proj_T(n, act, T["xC", b] + T["ctxsplitC", b])
                for k in range(2):
                    a = AC.op(lambda e, i=i, k=k, ps=ps, n=n: e.activation(qp[:, i, k, :], ps[:, k * 256:(k + 1) * 256], ACT.Identity,
                              bias=vec[:, VEC[n] + k:VEC[n] + k + 1]), tok + W("rope", b - 1) + end1)
                release(bs, a)
            moves = []
            src = qp[:, :, :, :].rearrange("p i k n -> p (i k n)")
            dst = qr[:, :, :, :].rearrange("p i k n -> p (i k n)")
            for w in range(2):
                moves.append((dst[64 * w:64 * w + 64, :], src[64 - 64 * w:128 - 64 * w, :]))
            T["qp", b] = a
            T["qr", b] = dma(moves, a + W("rope", b - 1))
            bs, ps, tok = proj_N("wv", C, [])
            T["projC", b] = tok
            a = AC.op(lambda e: e.activation(vv[b % 3][:, :, :, 0:16], ps.rearrange("p (t h d) -> p t h d", t=2, d=16), ACT.Copy),
                      tok + W("PV", b - 3) + k2)
            release(bs, a)
            T["vv", b] = a

        def C2(b):
            w = T["qp", b] + T["qr", b] + c_iota
            r = []
            for i, Q in ((0, VE), (1, VE)):
                cosb = rope[:, 0:1, :].broadcast_to([128, 2, 256])
                sinb = rope[:, 1:2, :].broadcast_to([128, 2, 256])
                a = Q.op(lambda e: e.tensor_tensor(qt[:, i, :, :], qp[:, i, :, :], cosb, ALU.mult), w)
                c = PO.op(lambda e: e.tensor_tensor(qr[:, i, :, :], qr[:, i, :, :], sinb, ALU.mult), w)
                a = Q.op(lambda e: e.tensor_tensor(qt[:, i, :, :], qt[:, i, :, :], qr[:, i, :, :], ALU.add), a + c)
                r += a
                f = W("stack", b - 1)
                c = AC.op(lambda e: e.activation(parts[:, i, 0, :, :], qt[:, i, :, :], ACT.Copy), a + f)
                a = Q.op(lambda e: e.tensor_tensor(qt[:, i, :, :], qt[:, i, :, :], parts[:, i, 0, :, :], ALU.subtract), a + c)
                c = AC.op(lambda e: e.activation(parts[:, i, 1, :, :], qt[:, i, :, :], ACT.Copy), a)
                a = Q.op(lambda e: e.tensor_tensor(parts[:, i, 2, :, :], qt[:, i, :, :], parts[:, i, 1, :, :], ALU.subtract), c + a)
                r += a
            T["rope", b] = r
            moves = []
            for i, order in enumerate([(0, 0, 0, 1, 1, 2), (0, 1, 2, 0, 1, 0)]):
                for c, p in enumerate(order):
                    moves.append((st_[b % 2][16 * c:16 * c + 16, i, :, :],
                                  parts[:, i, p, :, :].rearrange("p o n -> p (o n)")))
            T["stack", b] = dma(moves, r + W("PV", b - 2) + end1)

        mx = sb("mx", [128, 2, H])

        def C3(b):
            s = st_[b % 2]
            m = []
            for h in range(H):
                bs, ps, pw = mring.take()
                for t in range(2):
                    tok = PE.op(lambda e, t=t: e.matmul(ps[:, t * 256:(t + 1) * 256], s[0:96, 0, h, t * 128:(t + 1) * 128], s[0:96, 1, h, :],
                                                        start=True, stop=True), pw + T["stack", b] + k2, sig=(t == 1))
                    pw = []
                v = VE.op(lambda e: e.tensor_reduce(mpad[:, :, h:h + 1], ps.rearrange("p (a n) -> p a n", a=2), AX, ALU.max, negate=True),
                          tok + W("mT", b - 1) + k2)
                release(bs, v)
                m = v
            bs, ps, pw = gring.take()
            for t in range(2):
                tok = PE.op(lambda e, t=t: e.transpose(ps[:, t * 128:(t + 1) * 128], mpad[:, t, :], ident[:, :]), pw + m, sig=(t == 1))
                pw = []
            T["mT", b] = tok
            v = VE.op(lambda e: e.tensor_copy(mpt[:, 0, :], ps[0:16, 0:256]), tok + W("mrow", b - 1))
            v = VE.op(lambda e: e.tensor_tensor(mT[:, 0, :], ps[0:16, 0:256], mpt[:, 0, :], ALU.subtract), v)
            release(bs, v)
            v = VE.op(lambda e: e.tensor_copy(mpt[:, 1, :], mT[:, 0, :]), v)
            v = VE.op(lambda e: e.tensor_tensor(mpt[:, 2, :], mT[:, 0, :], mpt[:, 1, :], ALU.subtract), v)
            T["mrow", b] = dma([(s[96 + p:97 + p, 0, :, :], mpt[:, p, :]) for p in range(3)], v)

        def C4(b):
            s = st_[b % 2]
            for hg in range(4):
                etok = []
                slots = []
                for g in range(2):
                    bs, ps, pw = ering.take()
                    for j in range(2):
                        h = 4 * hg + 2 * g + j
                        for k in range(2):
                            tok = PE.op(lambda e, j=j, k=k, h=h, ps=ps: e.matmul(
                                ps[:, (2 * j + k) * 256:(2 * j + k + 1) * 256], s[0:99, 1, h, k * 128:(k + 1) * 128], s[0:99, 0, h, :],
                                start=True, stop=True), pw + T["mrow", b] + T["stack", b], sig=(j == 1 and k == 1))
                            pw = []
                    sl = (2 * hg + g) % 4
                    a = AC.op(lambda e, sl=sl, ps=ps: e.activation(PT[:, sl, :, :, :].rearrange("p a b n -> p (a b n)"), ps, ACT.Exp, scale=0.25),
                              tok + T.get(("PTfree", sl), []) + end1)
                    release(bs, a)
                    etok += a
                    slots.append(sl)
                if hg % 2 == 0:
                    obs, ops_, ow = gring.take()
                for k in range(2):
                    for j in range(4):
                        h = 4 * hg + j
                        tok = PE.op(lambda e, j=j, k=k, h=h, o=ops_, c=(hg % 2) * 256: e.matmul(
                            o[32 * j:32 * j + 32, c:c + 256], vv[b % 3][:, k, h, :], PT[:, slots[j // 2], j % 2, k, :],
                            start=(k == 0), stop=(k == 1)), etok + ow + T["vv", b], sig=(j == 3 and k == 1))
                        ow = []
                for sl in slots:
                    T["PTfree", sl] = tok
                if hg % 2 == 1:
                    a = AC.op(lambda e, o=ops_, hg=hg: e.activation(OT[:, hg - 1:hg + 1, :].rearrange("p a n -> p (a n)"), o, ACT.Copy),
                              tok + W("OTt", b - 1))
                    release(obs, a)
            T["PV", b] = tok
            T["OT", b] = a

        def C5(b):
            for t in range(2):
                bs, ps, pw = gring.take()
                for hg in range(4):
                    tok = PE.op(lambda e, hg=hg, t=t, ps=ps: e.transpose(ps[:, hg * 128:(hg + 1) * 128], OT[:, hg, t * 128:(t + 1) * 128], ident[:, :]),
                                pw + T["OT", b], sig=(hg == 3))
                    pw = []
                pv = ps.rearrange("p (h d) -> p h d", d=32)
                v = VE.op(lambda e, t=t, pv=pv: e.reciprocal(rd[:, t, :].rearrange("p (h d) -> p h d", d=1), pv[:, :, 16:17]), tok)
                v = VE.op(lambda e, t=t, pv=pv: e.tensor_tensor(On[:, t, :].rearrange("p (h d) -> p h d", d=16), pv[:, :, 0:16],
                          rd[:, t, :].rearrange("p (h d) -> p h d", d=1).broadcast_to([128, H, 16]), ALU.mult), v + W("Ont", b - 1))
                release(bs, v)
            T["OTt", b] = tok
            T["On", b] = v

        def C6(b):
            bs, ps, tok = transpose4(On, T["On", b])
            T["Ont", b] = tok
            T["oT", b] = split(bs, ps, tok, *oT, W("wo", b - 1), bias=vec[:, VEC["wv"]:VEC["wv"] + 2])

        def C7(b):
            bs, ps, tok = proj_N("wo", oT, T["oT", b])
            T["wo", b] = tok
            X = xall[:, b, :, :].rearrange("p a n -> p (a n)")
            v = PO.op(lambda e: e.tensor_tensor(xall[:, b, :, :], xall[:, b, :, :], bo[:, :].rearrange("p (a n) -> p a n", a=1).broadcast_to([128, 2, 256]), ALU.add),
                      T["xC", b] + c_tbo)
            v = VE.op(lambda e: e.scalar_tensor_tensor(out=X, in0=ps, scalar=tg[:, 1:2], in1=X, op0=ALU.mult, op1=ALU.add), tok + v)
            release(bs, v)
            T["x3", b] = v

        stages = [C0, C1, C2, C3, C4, C5, C6, C7]
        for step in range(NB + len(stages) - 1):
            for s in reversed(range(len(stages))):
                if 0 <= step - s < NB:
                    stages[s](step - s)

        hh, hlo = wA[0][:, 4:8, :], wA[1][:, 4:8, :]
        x4 = [(ch, cl), (xh, xl)]
        G[0] = Ring(list(range(8)))
        wait_end = []
        T["lt", 99] = T["lt", NB - 1]

        def D0(b):
            T["xD", b] = norm_T(b, T["x3", b], *x4[b % 2], W("fc", b - 2) if b > 1 else T["projC", NB - 1])
            m, o = router(b + 100, 1, x4[b % 2], T["xD", b], False)
            v = VE.op(lambda e: e.tensor_tensor(rsm[:, :, 0], mx8[:, :, 0], mx8[:, :, 1], ALU.subtract), m)
            a = AC.op(lambda e: e.activation(rsm[:, :, 1], rsm[:, :, 0], ACT.Tanh, scale=0.5), v)
            v = VE.op(lambda e: e.tensor_scalar(rsm[:, :, 2], rsm[:, :, 1], htg[:, 3:4], htg[:, 3:4], ALU.mult, ALU.add), a)
            v2 = VE.op(lambda e: e.tensor_scalar(rsm[:, :, 3], rsm[:, :, 2], -1.0, tg[:, 3:4], ALU.mult, ALU.add), v)
            v = VE.op(lambda e: e.tensor_tensor(oh1[:, :, :], oh1[:, :, :], rsm[:, :, 2:3].broadcast_to([128, 2, 8]), ALU.mult), v + o)
            v2 = VE.op(lambda e: e.tensor_tensor(oh2[:, :, :], oh2[:, :, :], rsm[:, :, 3:4].broadcast_to([128, 2, 8]), ALU.mult), v2 + o)
            T["gatD", b] = VE.op(lambda e: e.tensor_tensor(gat[:, b % 2, :, :], oh1[:, :, :], oh2[:, :, :], ALU.add), v + v2 + W("x4", b - 2))

        def D1(b):
            X = x4[b % 2]
            acc = [T["gatD", b], T["gatD", b]]
            done = []

            def up(i):
                bs, ps, pw = G[0].take()
                pw = pw + T["xD", b] + wtok[f"f{i}"]
                for j in range(2):
                    for k in range(2):
                        tok = mm3(ps[:, j * 256:(j + 1) * 256], hl(base[f"f{i}"], lambda m: m[:, k * 256 + j * 128:k * 256 + j * 128 + 128]),
                                  hl(X, lambda a: a[:, k, :]), k == 0, k == 1, pw, sig=(j == 1 and k == 1))
                        pw = []
                T["fc", b] = tok
                n = 4 * b + i
                a = AC.op(lambda e: e.activation(cx[:, n % 2, :], ps, ACT.Gelu), tok + (W("h32", n - 2) if n > 1 else T["ctxsplitC", NB - 1]))
                release(bs, a)
                c = AC.op(lambda e: e.activation(hh[:, n % 4, :], cx[:, n % 2, :], ACT.Copy), a + (W("pj", n - 4) if n > 3 else endA))
                T["h32", n] = VE.op(lambda e: e.tensor_tensor(hlo[:, n % 4, :], cx[:, n % 2, :], hh[:, n % 4, :].bitcast(F32), ALU.subtract), a + c)

            def down(i):
                n = 4 * b + i
                for j in range(2):
                    x_ = 2 * i + j
                    bs, ps, pw = G[0].take()
                    pw = pw + T["h32", n] + wtok[f"p{i}"]
                    for t in range(2):
                        tok = mm3(ps[:, t * 256:(t + 1) * 256], hl((hh, hlo), lambda m: m[:, n % 4, j * 256 + t * 128:j * 256 + t * 128 + 128]),
                                  hl(base[f"p{i}"], lambda m: m[:, j * 256:(j + 1) * 256]), True, True, pw, sig=(t == 1))
                        pw = []
                    for t in range(2):
                        acc[t] = VE.op(lambda e, t=t, ps=ps, x_=x_: e.scalar_tensor_tensor(
                            out=xall[:, b, t, :], in0=ps[:, t * 256:(t + 1) * 256], scalar=gat[:, b % 2, t, x_:x_ + 1],
                            in1=xall[:, b, t, :], op0=ALU.mult, op1=ALU.add), tok + acc[t] + T["x3", b])
                    release(bs, acc[0] + acc[1])
                T["pj", n] = tok

            up(0)
            up(1)
            for i in range(4):
                down(i)
                if i + 2 < 4:
                    up(i + 2)
            T["x4", b] = acc[0] + acc[1]
            wait_end.extend(dma([(out_d[b], xall[:, b, :, :])], T["x4", b]))

        stages = [D0, D1]
        for step in range(NB + len(stages) - 1):
            for s in reversed(range(len(stages))):
                if 0 <= step - s < NB:
                    stages[s](step - s)

        for s, v in wait_end:
            nc.sync.wait_ge(s, v)


def tables():
    inv = 1.0 / 10000.0 ** (np.arange(0, 16, 2, dtype=np.float32) / np.float32(16))
    f = np.arange(S, dtype=np.float32)[:, None] * inv[None, :].astype(np.float32)
    emb = np.concatenate([f, f], -1).astype(np.float32)
    cos, sin = np.cos(emb).T, np.sin(emb).T
    sin = np.concatenate([-sin[:8], sin[8:]], 0)
    rope = np.stack([np.repeat(cos, 8, 0), np.repeat(sin, 8, 0)], 1).astype(np.float32)
    iota = np.tile(np.arange(8, dtype=np.float32), (128, 1))
    return np.ascontiguousarray(rope), iota, np.eye(128, dtype=np.float32)


def kernel(**inputs):
    import concourse.bacc as _bacc
    from concourse.bass_utils import run_bass_kernel_spmd as _run

    a = {k: np.asarray(v) for k, v in inputs.items()}

    def heads(w):
        return w.reshape((8, 2, 16) + w.shape[1:]).swapaxes(0, 1).swapaxes(1, 2).reshape(w.shape)

    for n in ("Wq", "bq", "Wk", "bk"):
        a["L1_xattn_" + n] = heads(a["L1_xattn_" + n])

    def km(w):
        return w.T.reshape(-1, 128, w.shape[0]).transpose(1, 0, 2)

    mats = [km(a[n]).reshape(128, 512) for n in ["L0_xattn_Wq_c", "L0_xattn_Wk_c", "L0_xattn_Wq_s", "L0_xattn_Wk_s",
                                                 "L0_xattn_Wv_s", "L0_xattn_Wv_c"]]
    g = km(a["L0_xattn_Wg"])
    mats += [g[:, 0:2].reshape(128, 512), g[:, 2:4].reshape(128, 512)]
    mats += [km(a["L0_ffn_expert_w"][i]).reshape(128, 512) for i in range(8)]
    r = np.zeros((128, 2, 2, 128), np.float32)
    r[:, 0, :, 0:8] = km(a["L0_ffn_router_w"])
    r[:, 1, :, 0:8] = km(a["L1_ffn_w_gate"])
    mats += [r.reshape(128, 512)]
    mats += [km(a[n]).reshape(128, 512) for n in ["L1_xattn_Wq", "L1_xattn_Wk", "L1_xattn_Wv", "L1_xattn_Wo"]]
    fc = a["L1_ffn_w_fc"].reshape(4, 256, 256)
    mats += [km(fc[i]).reshape(128, 512) for i in range(4)]
    pj = a["L1_ffn_w_proj"].transpose(2, 0, 1).reshape(128, 4, 512)
    mats += [pj[:, i] for i in range(4)]
    vec = np.zeros((128, 22), np.float32)
    for i, n in enumerate(["L0_xattn_bq_c", "L0_xattn_bk_c", "L0_xattn_bq_s", "L0_xattn_bk_s", "L0_xattn_bv_s", "L0_xattn_bv_c",
                           "L0_xattn_bg", "L1_xattn_bq", "L1_xattn_bk", "L1_xattn_bv"]):
        vec[:, 2 * i:2 * i + 2] = a[n].reshape(2, 128).T
    vec[0:8, 20] = a["L0_ffn_router_b"]
    eb = np.zeros((128, 256), np.float32)
    eb[0:8] = a["L0_ffn_expert_b"]
    gg = np.tile(np.concatenate([a["g_xattn"], a["g_ffn"]]), (128, 1))
    rope, iota, ident = tables()
    arrays = {
        "x_d": a["x"].reshape(8, 2, 128, 256).transpose(0, 2, 1, 3),
        "ctx_d": a["ctx_1024"].transpose(0, 2, 1).reshape(8, 2, 128, 256).transpose(0, 2, 1, 3).reshape(8, 128, 512),
        "mats_d": np.stack(mats, 1), "vec_d": vec, "bo_d": np.tile(a["L1_xattn_bo"], (128, 1)), "g_d": gg, "eb_d": eb,
        "rope_d": rope, "iota_d": iota, "id_d": ident,
    }
    arrays = {k: np.ascontiguousarray(v) for k, v in arrays.items()}
    nc = _bacc.Bacc("TRN2", target_bir_lowering=False, num_devices=1)
    args = [nc.dram_tensor(k, v.shape, F32, kind="ExternalInput").ap() for k, v in arrays.items()]
    args.append(nc.dram_tensor("out_d", (8, 128, 2, 256), F32, kind="ExternalOutput").ap())
    flamingo(nc, *args)
    res = _run(nc, [arrays], core_ids=[0])
    return res.results[0]["out_d"].reshape(8, 128, 2, 256).transpose(0, 2, 1, 3).reshape(8, 256, 256)
```

```python
from contextlib import ExitStack

import numpy as np

import concourse.bass as bass
from concourse import mybir

F32 = mybir.dt.float32
F32R = mybir.dt.float32r
BF16 = mybir.dt.bfloat16
U32 = mybir.dt.uint32
ALU = mybir.AluOpType
ACT = mybir.ActivationFunctionType
AX = mybir.AxisListType.X

NB = 8
S = 256
D = 256
E = 8
H = 16
EPS = 1e-5

MATS = ["qc", "kc", "qs", "ks", "vs", "vc", "g0", "g1"] + [f"e{i}" for i in range(8)] + \
       ["r"] + ["wq", "wk", "wv", "wo"] + [f"f{i}" for i in range(4)] + [f"p{i}" for i in range(4)]
MI = {n: i for i, n in enumerate(MATS)}
VEC = {n: 2 * i for i, n in enumerate(["qc", "kc", "qs", "ks", "vs", "vc", "g", "wq", "wk", "wv", "rb"])}


class Queue:

    def __init__(self, eng, sem, serial=False):
        self.eng, self.sem, self.n, self.seen, self.serial = eng, sem, 0, {}, serial

    def op(self, fn, waits=(), sig=True):
        if self.serial and self.n:
            waits = list(waits) + [(self.sem, self.n)]
        need = {}
        for sem, v in waits:
            if v > self.seen.get(id(sem), 0):
                self.seen[id(sem)] = v
                need[id(sem)] = (sem, v)
        for sem, v in need.values():
            self.eng.wait_ge(sem, v)
        i = fn(self.eng)
        if not sig:
            return []
        i.then_inc(self.sem, 1)
        self.n += 1
        return [(self.sem, self.n)]


def flamingo(nc, x_d, ctx_d, mats_d, vec_d, bo_d, g_d, eb_d, rope_d, iota_d, id_d, out_d):
    with ExitStack() as st:
        def sb(name, shape, dt=F32):
            return st.enter_context(nc.sbuf_tensor(name, shape, dt))

        nsem = [0]

        def sem():
            nsem[0] += 1
            return st.enter_context(nc.semaphore(f"s{nsem[0]}"))

        PE, AC, VE, SP = (Queue(e, sem()) for e in (nc.tensor, nc.scalar, nc.vector, nc.sync))
        PO = Queue(nc.gpsimd, sem(), serial=True)

        def dma(parts, waits=(), q=None):
            q = q or SP
            s = sem()
            for i, (o, a) in enumerate(parts):
                q.op(lambda e, o=o, a=a: e.dma_start(o, a).then_inc(s, 16), waits if i == 0 else (), sig=False)
            return [(s, 16 * len(parts))]

        T = {}

        def W(name, b):
            return T[name, b] if b >= 0 else []

        xall = sb("xall", [128, NB, 2, 256])
        vec = sb("vec", [128, 22])
        gb = sb("gb", [128, 4])
        tg = sb("tg", [128, 4])
        htg = sb("htg", [128, 4])
        hbg = sb("hbg", [128, 2])
        bo = sb("bo", [128, 256])
        rope = sb("rope", [128, 2, 256])
        iota = sb("iota", [128, 8])
        ident = sb("ident", [128, 128])
        nhalf = sb("nhalf", [128, 2])
        stage = sb("stage", [128, 4, 512])
        wr_h = sb("wr_h", [128, 512], F32R)
        wr_l = sb("wr_l", [128, 512], F32R)
        wA = [sb(f"wA{i}", [128, 8, 512], F32R) for i in range(2)]
        wB = [sb(f"wB{i}", [128, 8, 512], F32R) for i in range(2)]
        base = {}
        for i, n in enumerate(MATS):
            if n == "r":
                base[n] = (wr_h[:, :], wr_l[:, :])
            else:
                j = i if i < 16 else i - 17
                reg = wA if (i < 8 or 17 <= i < 21) else wB
                k = i if i < 8 else (i - 8 if i < 16 else (i - 17 if i < 21 else i - 21))
                base[n] = (reg[0][:, k, :], reg[1][:, k, :])
        xn = sb("xn", [128, 2, 2, 256])
        stt = sb("stt", [128, 2, 2, 6])
        mv = sb("mv", [128, 2, 2, 2])
        ve = sb("ve", [128, 2])
        rstd = sb("rstd", [128, 2, 2])
        xh = sb("xh", [128, 2, 256], F32R)
        xl = sb("xl", [128, 2, 256], F32R)
        lt = sb("lt", [128, 256])
        lg = sb("lg", [128, 2, 8])
        mx8 = sb("mx8", [128, 2, 8])
        ix8 = sb("ix8", [128, 2, 8], U32)
        ixf = sb("ixf", [128, 2, 8])
        oh1 = sb("oh1", [128, 2, 8])
        oh2 = sb("oh2", [128, 2, 8])
        rex = sb("rex", [128, 2, 8])
        rsm = sb("rsm", [128, 2, 4])
        gat = sb("gat", [128, 2, 2, 8])
        cx = sb("cx", [128, 2, 512])
        ch = sb("ch", [128, 2, 256], F32R)
        cl = sb("cl", [128, 2, 256], F32R)
        psum = st.enter_context(nc.psum_tensor("psum", [128, 8, 512], F32))
        bank_free = [[] for _ in range(8)]

        class Ring:
            def __init__(self, banks, width=1):
                self.banks, self.width, self.at = banks, width, 0

            def take(self):
                k = (self.at * self.width) % len(self.banks)
                self.at += 1
                bs = self.banks[k:k + self.width]
                waits = [t for b in bs for t in bank_free[b]]
                for b in bs:
                    bank_free[b] = None
                return bs, psum[:, bs[0]:bs[0] + self.width, :].rearrange("p a n -> p (a n)"), waits

        def release(bs, toks):
            for b in bs:
                bank_free[b] = list(toks)

        def hl(pair, f):
            return f(pair[0]), f(pair[1])

        def mm3(out, lhs, rhs, start, stop, waits=(), sig=False):
            seq = [(lhs[0], rhs[0]), (lhs[0], rhs[1]), (lhs[1], rhs[0])]
            tok = []
            for i, (a, m) in enumerate(seq):
                last = i == 2
                tok = PE.op(lambda e, a=a, m=m, i=i, last=last: e.matmul(out, a, m, start=start and i == 0, stop=stop and last),
                            waits if i == 0 else (), sig=sig and last)
            return tok

        ph1 = ExitStack()

        def s1(name, shape, dt=F32):
            return ph1.enter_context(nc.sbuf_tensor(name, shape, dt))

        pr = {n: (s1(n + "h", [128, 2, 256], F32R), s1(n + "l", [128, 2, 256], F32R)) for n in ["qc", "kc", "qs", "ks", "vs", "vc"]}
        P1 = [s1(f"P1{i}", [128, 2, 256]) for i in range(2)]
        PT1 = [(s1(f"PT{i}h", [128, 2, 256], F32R), s1(f"PT{i}l", [128, 2, 256], F32R)) for i in range(2)]
        sm = [s1(f"sm{i}", [128, 8]) for i in range(2)]
        cf = [s1(f"cf{i}", [128, 2, 256]) for i in range(2)]
        cs = [(s1(f"cs{i}h", [128, 2, 256], F32R), s1(f"cs{i}l", [128, 2, 256], F32R)) for i in range(2)]
        gt = s1("gt", [128, 2, 256])
        dd = s1("dd", [128, 2, 256])
        uu = s1("uu", [128, 2, 256])
        mxn = s1("mxn", [128, 2, 256])
        x2 = [(s1(f"x2h{i}", [128, 2, 256], F32R), s1(f"x2l{i}", [128, 2, 256], F32R)) for i in range(2)]
        C, X = (ch, cl), (xh, xl)
        ebh = s1("ebh", [128, 256], F32R)
        ebl = s1("ebl", [128, 256], F32R)
        gpad = s1("gpad", [128, 2, 128])
        gTh = s1("gTh", [128, 256], F32R)
        gTl = s1("gTl", [128, 256], F32R)

        c_vec = dma([(vec[:, :], vec_d)])
        c_id = dma([(ident[:, :], id_d)])
        c_g = dma([(gb[:, :], g_d)])
        tok_x = {}
        for b in range(NB):
            pass

        def load_ctx(name, b, waits):
            T["cx", name, b] = dma([(cx[:, b % 2, :], ctx_d[b])], waits)

        PO.op(lambda e: e.memset(nhalf[:, :], -0.5))
        c_nh = PO.op(lambda e: e.memset(gpad[:, :, :], 0.0))
        c_tg = AC.op(lambda e: e.activation(tg[:, :], gb[:, :], ACT.Tanh), c_g)
        c_hbg = VE.op(lambda e: e.tensor_scalar(hbg[:, :], vec[:, VEC["g"]:VEC["g"] + 2], 0.5, None, ALU.mult), c_vec)

        for b in range(2):
            load_ctx("A", b, ())
            T["x", b] = dma([(xall[:, b, :, :], x_d[b])])
        stage_free = [[] for _ in range(4)]
        wtok = {}
        nst = [0]

        def load_mat(n, waits=()):
            k = nst[0] % 4
            nst[0] += 1
            t = dma([(stage[:, k, :], mats_d[:, MI[n], :])], stage_free[k])
            h, l = base[n]
            a = AC.op(lambda e: e.activation(h, stage[:, k, :], ACT.Copy), t + list(waits))
            v = VE.op(lambda e: e.tensor_tensor(l, stage[:, k, :], h.bitcast(F32), ALU.subtract), a + t)
            stage_free[k] = v
            wtok[n] = v

        mv_free, xn_free = [[], []], [[], []]
        ring = Ring(list(range(8)))
        G = [ring]
        rt_free = {"lt": []}

        def ln_stats(name, b, x_tok):
            i = "ABCD".index(name) % 2
            s = []
            for t in range(2):
                s += VE.op(lambda e: e.bn_stats(stt[:, i, t, :], xall[:, b, t, :]), x_tok)
            a = []
            for t in range(2):
                a += VE.op(lambda e: e.bn_aggr(mv[:, i, t, :], stt[:, i, t, :]), s + mv_free[i])
            p = PO.op(lambda e: e.tensor_scalar(ve[:, :], mv[:, i, :, 1], EPS, None, ALU.add), a + c_nh)
            T["rstd" + name, b] = a + PO.op(lambda e: e.tensor_tensor(rstd[:, i, :], ve[:, :], nhalf[:, :], ALU.pow), p + mv_free[i])

        def ln_apply(name, b):
            i = "ABCD".index(name) % 2
            n = []
            for t in range(2):
                n += VE.op(lambda e: e.tensor_scalar(xn[:, i, t, :], xall[:, b, t, :], mv[:, i, t, 0:1],
                                                     rstd[:, i, t:t + 1], ALU.subtract, ALU.mult), T["rstd" + name, b] + xn_free[i])
            mv_free[i] = n
            T["xn" + name, b] = n

        def ln_T(name, b, h, l, used):
            i = "ABCD".index(name) % 2
            bs, ps, tok = transpose4(xn[:, i, :, :], T["xn" + name, b])
            xn_free[i] = tok
            T["xT" + name, b] = split(bs, ps, tok, h, l, used)

        def transpose4(src, toks):
            bs, ps, w = G[0].take()
            for k in range(2):
                for t in range(2):
                    tok = PE.op(lambda e, k=k, t=t: e.transpose(ps[:, k * 256 + t * 128:k * 256 + t * 128 + 128],
                                                               src[:, t, k * 128:(k + 1) * 128], ident[:, :]),
                                w + list(toks) + c_id, sig=(k == 1 and t == 1))
                    w = []
            return bs, ps, tok

        def split(bs, ps, tok, h, l, free, bias=None):
            hf, lf = h.rearrange("p a n -> p (a n)"), l.rearrange("p a n -> p (a n)")
            if bias is None:
                a = AC.op(lambda e: e.activation(hf, ps, ACT.Copy), tok + list(free))
                v = VE.op(lambda e: e.tensor_tensor(lf, ps, hf.bitcast(F32), ALU.subtract), a)
            else:
                for k in range(2):
                    a = AC.op(lambda e, k=k: e.activation(h[:, k, :], ps[:, k * 256:(k + 1) * 256], ACT.Identity,
                                                          bias=bias[:, k:k + 1]), tok + list(free) + c_vec)
                for k in range(2):
                    v = VE.op(lambda e, k=k: e.scalar_tensor_tensor(
                        out=l[:, k, :], in0=ps[:, k * 256:(k + 1) * 256], scalar=bias[:, k:k + 1],
                        in1=h[:, k, :].bitcast(F32), op0=ALU.add, op1=ALU.subtract), a)
            release(bs, v)
            return v

        def proj_T(w, act, waits):
            bs, ps, pw = G[0].take()
            pw = pw + list(waits) + wtok[w]
            for o in range(2):
                for k in range(2):
                    tok = mm3(ps[:, o * 256:(o + 1) * 256], hl(base[w], lambda m: m[:, k * 256 + o * 128:k * 256 + o * 128 + 128]),
                              hl(act, lambda a: a[:, k, :]), k == 0, k == 1, pw, sig=(o == 1 and k == 1))
                    pw = []
            return bs, ps, tok

        def proj_N(w, act, waits):
            bs, ps, pw = G[0].take()
            pw = pw + list(waits) + wtok[w]
            for t in range(2):
                for k in range(2):
                    tok = mm3(ps[:, t * 256:(t + 1) * 256], hl(act, lambda a: a[:, k, t * 128:(t + 1) * 128]),
                              hl(base[w], lambda m: m[:, k * 256:(k + 1) * 256]), k == 0, k == 1, pw, sig=(t == 1 and k == 1))
                    pw = []
            return bs, ps, tok

        def router_mm(name, b, half, act):
            bs, ps, pw = G[0].take()
            pw = pw + T["xT" + name, b] + wtok["r"]
            for k in range(2):
                tok = mm3(ps[:, 0:256], hl(base["r"], lambda m: m[:, half * 256 + k * 128:half * 256 + k * 128 + 128]),
                          hl(act, lambda a: a[:, k, :]), k == 0, k == 1, pw, sig=(k == 1))
                pw = []
            if half == 0:
                a = AC.op(lambda e: e.activation(lt[0:8, :], ps[0:8, 0:256], ACT.Identity, bias=vec[0:8, VEC["rb"]:VEC["rb"] + 1]),
                          tok + rt_free["lt"])
            else:
                a = AC.op(lambda e: e.activation(lt[0:8, :], ps[0:8, 0:256], ACT.Copy), tok + rt_free["lt"])
            release(bs, a)
            T["lt" + name, b] = a

        def router_top(name, b, n):
            bs, ps, pw = G[0].take()
            pw = pw + T["lt" + name, b]
            for t in range(2):
                tok = PE.op(lambda e: e.transpose(ps[:, t * 8:t * 8 + 8], lt[0:8, t * 128:(t + 1) * 128], ident[0:8, 0:8]),
                            pw, sig=(t == 1))
                pw = []
            rt_free["lt"] = tok
            v = VE.op(lambda e: e.tensor_copy(lg[:, :, :].rearrange("p a n -> p (a n)"), ps[:, 0:16]), tok)
            release(bs, v)
            m, i = [], []
            for t in range(2):
                m += VE.op(lambda e: e.max(mx8[:, t, :], lg[:, t, :]), v)
            for t in range(2):
                i += VE.op(lambda e: e.max_index(ix8[:, t, :], mx8[:, t, :], lg[:, t, :]), m)
            f = VE.op(lambda e: e.tensor_copy(ixf[:, :, :], ix8[:, :, :]), i + c_iota)
            o = []
            for t in range(2):
                for oh, c in ((oh1, 0), (oh2, 1))[:n]:
                    o += VE.op(lambda e: e.tensor_scalar(oh[:, t, :], iota[:, :], ixf[:, t, c:c + 1], None, ALU.is_equal), f)
            return m, o

        def a_load(b):
            if b < NB:
                load_ctx("A", b, W("ctxsplitA", b - 2))
                T["x", b] = dma([(xall[:, b, :, :], x_d[b])])

        def ctx_split(name, b, free):
            cf_ = cx[:, b % 2, :]
            a = AC.op(lambda e: e.activation(ch[:, :, :].rearrange("p a n -> p (a n)"), cf_, ACT.Copy), T["cx", name, b] + free)
            T["ctxsplit" + name, b] = PO.op(lambda e: e.tensor_tensor(cl[:, :, :].rearrange("p a n -> p (a n)"), cf_,
                                            ch[:, :, :].rearrange("p a n -> p (a n)").bitcast(F32), ALU.subtract), a + free)

        def a_stats(b):
            ln_stats("A", b, T["x", b])

        def a_apply(b):
            ln_apply("A", b)

        def a_norm(b):
            f = W("projA", b - 1)
            ln_T("A", b, xh, xl, f)
            ctx_split("A", b, f)
            a_load(b + 2)

        def a_proj(*names):
            def run(b):
                for n in names:
                    act, tr = {"qc": (X, 1), "ks": (C, 1), "qs": (C, 1), "kc": (X, 1), "vs": (C, 0), "vc": (X, 0)}[n]
                    bs, ps, tok = (proj_T if tr else proj_N)(n, act, T["xTA", b] + T["ctxsplitA", b])
                    free = W({"qc": "S0", "ks": "S0", "qs": "S1", "kc": "S1", "vs": "PV0", "vc": "PV1"}[n], b - 1)
                    T[n, b] = split(bs, ps, tok, *pr[n], free, bias=vec[:, VEC[n]:VEC[n] + 2] if tr else None)
                    T["projA", b] = tok
            return run

        def a_scores(i):
            q, k = [("qc", "ks"), ("qs", "kc")][i]
            s = sm[i]

            def run(b):
                bs, ps, pw = G[0].take()
                pw = pw + T[q, b] + T[k, b]
                for t in range(2):
                    for kk in range(2):
                        tok = mm3(ps[:, t * 256:(t + 1) * 256], hl(pr[q], lambda m: m[:, kk, t * 128:(t + 1) * 128]),
                                  hl(pr[k], lambda m: m[:, kk, :]), kk == 0, kk == 1, pw, sig=(t == 1 and kk == 1))
                        pw = []
                T[f"S{i}", b] = tok
                v = VE.op(lambda e: e.tensor_reduce(s[:, 0:2], ps.rearrange("p (a n) -> p a n", a=2), AX, ALU.max, negate=True), tok + W(f"P{i}", b - 1))
                v = VE.op(lambda e: e.tensor_scalar(s[:, 2:4], s[:, 0:2], 1.0 / 16, None, ALU.mult), v)
                for t in range(2):
                    a = AC.op(lambda e: e.activation(P1[i][:, t, :], ps[:, t * 256:(t + 1) * 256], ACT.Exp, bias=s[:, 2 + t:3 + t],
                                                     scale=1.0 / 16, accum_out=s[:, 4 + t:5 + t]), v + W(f"PTt{i}", b - 1))
                release(bs, a)
                T[f"E{i}", b] = a
            return run

        def a_scale(i):
            s = sm[i]

            def run(b):
                v = VE.op(lambda e: e.reciprocal(s[:, 6:8], s[:, 4:6]), T[f"E{i}", b])
                r = []
                for t in range(2):
                    r += VE.op(lambda e: e.tensor_scalar(P1[i][:, t, :], P1[i][:, t, :], s[:, 6 + t:7 + t], None, ALU.mult), v)
                T[f"P{i}", b] = r
            return run

        def a_PT(i):
            def run(b):
                bs, ps, tok = transpose4(P1[i], T[f"P{i}", b])
                T[f"PTt{i}", b] = tok
                T[f"PT{i}", b] = split(bs, ps, tok, *PT1[i], W(f"PV{i}", b - 1))
            return run

        def a_PV(i):
            v_ = ["vs", "vc"][i]

            def run(b):
                bs, ps, pw = G[0].take()
                pw = pw + T[f"PT{i}", b] + T[v_, b]
                for o in range(2):
                    for k in range(2):
                        tok = mm3(ps[:, o * 256:(o + 1) * 256], hl(pr[v_], lambda m: m[:, k, o * 128:(o + 1) * 128]),
                                  hl(PT1[i], lambda m: m[:, k, :]), k == 0, k == 1, pw, sig=(o == 1 and k == 1))
                        pw = []
                T[f"PV{i}", b] = tok
                bias = vec[:, VEC[v_]:VEC[v_] + 2]
                for k in range(2):
                    a = AC.op(lambda e: e.activation(cf[i][:, k, :], ps[:, k * 256:(k + 1) * 256], ACT.Identity, bias=bias[:, k:k + 1]),
                              tok + W("uu", b - 1))
                release(bs, a)
                v = VE.op(lambda e: e.tensor_copy(cs[i][0][:, :, :], cf[i][:, :, :]), a + W("gate", b - 1))
                T[f"cs{i}", b] = PO.op(lambda e: e.tensor_tensor(cs[i][1][:, :, :], cf[i][:, :, :], cs[i][0][:, :, :].bitcast(F32), ALU.subtract), v)
            return run

        def a_gate(b):
            bs, ps, pw = G[0].take()
            pw = pw + T["cs0", b] + T["cs1", b] + wtok["g0"] + wtok["g1"]
            for o in range(2):
                for k in range(4):
                    tok = mm3(ps[:, o * 256:(o + 1) * 256], hl(base[f"g{k // 2}"], lambda m: m[:, (k % 2) * 256 + o * 128:(k % 2) * 256 + o * 128 + 128]),
                              hl(cs[k // 2], lambda m: m[:, k % 2, :]), k == 0, k == 3, pw, sig=(o == 1 and k == 3))
                    pw = []
            T["gate", b] = tok
            p = PO.op(lambda e: e.tensor_tensor(dd[:, :, :], cf[0][:, :, :], cf[1][:, :, :], ALU.subtract), T["cs0", b] + T["cs1", b] + W("uu", b - 1))
            v1 = PO.op(lambda e: e.tensor_tensor(uu[:, :, :], cf[0][:, :, :], cf[1][:, :, :], ALU.add), p + W("mixT", b - 1))
            for k in range(2):
                a = AC.op(lambda e: e.activation(gt[:, k, :], ps[:, k * 256:(k + 1) * 256], ACT.Tanh, bias=hbg[:, k:k + 1], scale=0.5),
                          tok + c_hbg + W("uu", b - 1))
            release(bs, a)
            v = VE.op(lambda e: e.tensor_tensor(dd[:, :, :], dd[:, :, :], gt[:, :, :], ALU.mult), a + p)
            T["uu", b] = VE.op(lambda e: e.tensor_tensor(uu[:, :, :], uu[:, :, :], dd[:, :, :], ALU.add), v + v1)

        def a_mix(b):
            bs, ps, pw = G[0].take()
            pw = pw + T["uu", b]
            for t in range(2):
                for k in range(2):
                    tok = PE.op(lambda e: e.transpose(ps[:, t * 256 + k * 128:t * 256 + k * 128 + 128], uu[:, k, t * 128:(t + 1) * 128],
                                                      ident[:, :]), pw, sig=(t == 1 and k == 1))
                    pw = []
            T["mixT", b] = tok
            xb = xall[:, b, :, :].rearrange("p a n -> p (a n)")
            v = VE.op(lambda e: e.scalar_tensor_tensor(out=xb, in0=ps, scalar=htg[:, 0:1], in1=xb, op0=ALU.mult, op1=ALU.add), tok + c_htg)
            release(bs, v)
            T["x1", b] = v
            ln_stats("B", b, v)

        def b_apply(b):
            ln_apply("B", b)

        def b_norm(b):
            ln_T("B", b, *x2[b % 2], W("exp", b - 2))

        def b_route(b):
            router_mm("B", b, 0, x2[b % 2])

        def b_top(b):
            m, o = router_top("B", b, 1)
            v = VE.op(lambda e: e.tensor_tensor(rex[:, :, :], lg[:, :, :], mx8[:, :, 0:1].broadcast_to([128, 2, 8]), ALU.subtract), m)
            a = AC.op(lambda e: e.activation(rex[:, :, :], rex[:, :, :], ACT.Exp), v)
            v = VE.op(lambda e: e.reduce_sum(rsm[:, :, 0], rex[:, :, :], axis=AX), a)
            v = VE.op(lambda e: e.reciprocal(rsm[:, :, 1], rsm[:, :, 0]), v)
            v = VE.op(lambda e: e.tensor_scalar(rsm[:, :, 2], rsm[:, :, 1], tg[:, 2:3], None, ALU.mult), v + c_tg)
            v = VE.op(lambda e: e.tensor_tensor(gat[:, b % 2, :, :], oh1[:, :, :], rsm[:, :, 2:3].broadcast_to([128, 2, 8]), ALU.mult), v + o + W("x2", b - 2))
            T["gat", b] = v
            T["gpad", b] = VE.op(lambda e: e.tensor_copy(gpad[:, :, 0:8], gat[:, b % 2, :, :]), v + W("gTt", b - 1) + c_nh)

        def b_gT(b):
            bs, ps, pw = G[0].take()
            for t in range(2):
                tok = PE.op(lambda e: e.transpose(ps[:, t * 128:(t + 1) * 128], gpad[:, t, :], ident[:, :]), pw + T["gpad", b], sig=(t == 1))
                pw = []
            T["gTt", b] = tok
            a = AC.op(lambda e: e.activation(gTh[:, :], ps[:, 0:256], ACT.Copy), tok + W("bias", b - 1))
            v = VE.op(lambda e: e.tensor_tensor(gTl[:, :], ps[:, 0:256], gTh[:, :].bitcast(F32), ALU.subtract), a)
            release(bs, v)
            T["gT", b] = v

        def b_bias(b):
            bs, ps, pw = G[0].take()
            pw = pw + T["gT", b] + c_eb
            for t in range(2):
                tok = mm3(ps[:, t * 256:(t + 1) * 256], hl((gTh, gTl), lambda m: m[:, t * 128:(t + 1) * 128]), (ebh[:, :], ebl[:, :]), True, True, pw, sig=(t == 1))
                pw = []
            T["bias", b] = tok
            xb = xall[:, b, :, :].rearrange("p a n -> p (a n)")
            v = VE.op(lambda e: e.tensor_tensor(xb, ps, xb, ALU.add), tok)
            release(bs, v)
            acc[b] = [v, v]

        acc = {}

        def weigh(b, bs, ps, tok, x_):
            for t in range(2):
                acc[b][t] = VE.op(lambda e: e.scalar_tensor_tensor(
                    out=xall[:, b, t, :], in0=ps[:, t * 256:(t + 1) * 256], scalar=gat[:, b % 2, t, x_:x_ + 1],
                    in1=xall[:, b, t, :], op0=ALU.mult, op1=ALU.add), tok + acc[b][t])
            release(bs, acc[b][0] + acc[b][1])

        def b_expert(x_):
            def run(b):
                if x_ == 0:
                    b_bias(b)
                bs, ps, tok = proj_N(f"e{x_}", x2[b % 2], T["gat", b])
                weigh(b, bs, ps, tok, x_)
                T["exp", b] = tok
                T["x2", b] = acc[b][0] + acc[b][1]
            return run

        for n in ["qc", "ks", "qs", "kc", "vs", "vc"]:
            load_mat(n)
        c_htg = VE.op(lambda e: e.tensor_scalar(htg[:, :], tg[:, :], 0.5, None, ALU.mult), c_tg)
        load_mat("g0")
        load_mat("g1")
        load_mat("r")
        ek = nst[0] % 4
        nst[0] += 1
        c_iota = dma([(iota[:, :], iota_d), (stage[:, ek, 0:256], eb_d), (bo[:, :], bo_d), (rope[:, :, :], rope_d)], stage_free[ek])
        t_ = AC.op(lambda e: e.activation(ebh[:, :], stage[:, ek, 0:256], ACT.Copy), c_iota)
        c_eb = VE.op(lambda e: e.tensor_tensor(ebl[:, :], stage[:, ek, 0:256], ebh[:, :].bitcast(F32), ALU.subtract), t_)
        stage_free[ek] = c_eb
        c_tbo = VE.op(lambda e: e.tensor_scalar(bo[:, :], bo[:, :], tg[:, 1:2], None, ALU.mult), c_iota + c_tg)
        for n in range(8):
            load_mat(f"e{n}")

        def pipeline(slots, first, last):
            for k in range(first, last):
                for lag, fn in slots:
                    if 0 <= k - lag < NB:
                        fn(k - lag)

        x_ = b_expert
        pipeline([
            (1, a_PV(0)), (2, x_(0)), (1, a_PV(1)), (-1, a_stats), (2, x_(1)), (1, a_gate), (0, a_proj("qc")), (2, x_(2)), (0, a_proj("ks")),
            (1, a_mix), (-1, a_apply), (2, x_(3)), (0, a_proj("qs")), (0, a_scores(0)), (1, b_apply), (0, a_proj("kc")), (0, a_scale(0)), (1, b_norm),
            (0, a_proj("vs")), (0, a_scores(1)), (2, x_(4)), (1, b_route), (0, a_PT(0)), (0, a_proj("vc")), (0, a_scale(1)), (2, x_(5)), (1, b_top),
            (-1, a_norm), (2, x_(6)), (0, a_PT(1)), (2, x_(7)), (1, b_gT),
        ], -1, NB + 2)
        ph1.close()
        endA = T["projA", NB - 1] + T["gate", NB - 1]
        endB = T["exp", NB - 1]
        end1 = T["x2", NB - 1] + endB + T["uu", NB - 1] + T["mixT", NB - 1] + T["bias", NB - 1]

        qp = sb("qp", [128, 2, 2, 256])
        qr = sb("qr", [128, 2, 2, 256])
        qt = sb("qt", [128, 2, 2, 256])
        parts = sb("parts", [128, 2, 3, 2, 256], BF16)
        st_ = [sb(f"st{i}", [99, 2, H, 256], BF16) for i in range(2)]
        vv = [sb(f"vv{i}", [128, 2, H, 32]) for i in range(3)]
        mpad = sb("mpad", [128, 2, 128])
        mT = sb("mT", [16, 2, 256])
        mpt = sb("mpt", [16, 3, 256], BF16)
        PT = sb("PT", [128, 6, 2, 256])
        x4 = (sb("x4h", [128, 2, 256], F32R), sb("x4l", [128, 2, 256], F32R))
        hh, hlo = wA[0][:, 4:8, :], wA[1][:, 4:8, :]
        OT = sb("OT", [128, 4, 256])
        rd = sb("rd", [128, 2, H])
        On = sb("On", [128, 2, 256])
        oT = (sb("oTh", [128, 2, 256], F32R), sb("oTl", [128, 2, 256], F32R))

        for n in ["wq", "wk", "wv", "wo"]:
            load_mat(n, endA)
        k2 = PO.op(lambda e: e.memset(mpad[:, :, :], 0.0), end1)
        for i in range(3):
            k2 = PO.op(lambda e, i=i: e.memset(vv[i][:, :, :, 16:32], 0.0), end1)
        for i in range(2):
            k2 = PO.op(lambda e, i=i: e.memset(st_[i][96:99, 1, :, :], 1.0), end1)
        for i in range(3):
            k2 = PO.op(lambda e, i=i: e.memset(vv[i][:, :, :, 16:17], 1.0), k2)
        for n in ["f0", "f1", "f2", "f3", "p0", "p1", "p2", "p3"]:
            load_mat(n, endB)
        gring, oring, mring, ering = Ring([0, 1, 2]), Ring([3]), Ring([4, 5]), Ring([6, 7])
        G[0] = gring

        def c_load(b):
            if b < NB:
                load_ctx("C", b, W("ctxsplitC", b - 2) if b > 1 else T["ctxsplitA", NB - 1])

        def c_stats(b):
            ln_stats("C", b, T["x2", b])

        def c_apply(b):
            ln_apply("C", b)

        def c_norm(b):
            f = W("projC", b - 1) if b else T["projA", NB - 1]
            ln_T("C", b, xh, xl, f)
            ctx_split("C", b, f)
            c_load(b + 2)

        def c_qk(b):
            for i, (n, act) in enumerate([("wq", X), ("wk", C)]):
                bs, ps, tok = proj_T(n, act, T["xTC", b] + T["ctxsplitC", b])
                for k in range(2):
                    a = AC.op(lambda e: e.activation(qp[:, i, k, :], ps[:, k * 256:(k + 1) * 256], ACT.Identity,
                              bias=vec[:, VEC[n] + k:VEC[n] + k + 1]), tok + W("rope", b - 1) + end1)
                release(bs, a)
            src = qp[:, :, :, :].rearrange("p i k n -> p (i k n)")
            dst = qr[:, :, :, :].rearrange("p i k n -> p (i k n)")
            T["qp", b] = a
            T["qr", b] = dma([(dst[64 * w:64 * w + 64, :], src[64 - 64 * w:128 - 64 * w, :]) for w in range(2)], a + W("rope", b - 1))

        def c_v(b):
            bs, ps, tok = proj_N("wv", C, [])
            T["projC", b] = tok
            a = AC.op(lambda e: e.activation(vv[b % 3][:, :, :, 0:16], ps.rearrange("p (t h d) -> p t h d", t=2, d=16), ACT.Copy),
                      tok + W("PV", b - 3) + k2)
            release(bs, a)
            T["vv", b] = a

        def c_rope(i):
            def run(b):
                w = T["qp", b] + T["qr", b] + c_iota
                a = VE.op(lambda e: e.tensor_tensor(qt[:, i, :, :], qp[:, i, :, :], rope[:, 0:1, :].broadcast_to([128, 2, 256]), ALU.mult), w)
                c = PO.op(lambda e: e.tensor_tensor(qr[:, i, :, :], qr[:, i, :, :], rope[:, 1:2, :].broadcast_to([128, 2, 256]), ALU.mult), w)
                a = VE.op(lambda e: e.tensor_tensor(qt[:, i, :, :], qt[:, i, :, :], qr[:, i, :, :], ALU.add), a + c)
                T["turn", i, b] = a
                c = AC.op(lambda e: e.activation(parts[:, i, 0, :, :], qt[:, i, :, :], ACT.Copy), a + W("stack", b - 1))
                a = PO.op(lambda e: e.tensor_tensor(qt[:, i, :, :], qt[:, i, :, :], parts[:, i, 0, :, :], ALU.subtract), a + c)
                T["part", i, b] = a
            return run

        def c_parts(b):
            r = []
            for i in range(2):
                a = T["part", i, b]
                c = AC.op(lambda e: e.activation(parts[:, i, 1, :, :], qt[:, i, :, :], ACT.Copy), a)
                r += PO.op(lambda e: e.tensor_tensor(parts[:, i, 2, :, :], qt[:, i, :, :], parts[:, i, 1, :, :], ALU.subtract), c + a)
            T["rope", b] = r

        def c_stack(b):
            moves = []
            for i, order in enumerate([(0, 0, 0, 1, 1, 2), (0, 1, 2, 0, 1, 0)]):
                for c, p in enumerate(order):
                    moves.append((st_[b % 2][16 * c:16 * c + 16, i, :, :],
                                  parts[:, i, p, :, :].rearrange("p o n -> p (o n)")))
            T["stack", b] = dma(moves, T["rope", b] + W("ST", b - 2) + W("mT", b - 2) + k2)

        def c_max(h):
            def run(b):
                s = st_[b % 2]
                bs, ps, pw = mring.take()
                for t in range(2):
                    tok = PE.op(lambda e: e.matmul(ps[:, t * 256:(t + 1) * 256], s[0:96, 0, h, t * 128:(t + 1) * 128], s[0:96, 1, h, :],
                                                   start=True, stop=True), pw + T["stack", b], sig=(t == 1))
                    pw = []
                v = VE.op(lambda e: e.tensor_reduce(mpad[:, :, h:h + 1], ps.rearrange("p (a n) -> p a n", a=2), AX, ALU.max, negate=True),
                          tok + W("mT", b - 1) + k2)
                release(bs, v)
                T["max", b] = v
            return run

        def c_maxT(b):
            s = st_[b % 2]
            bs, ps, pw = gring.take()
            for t in range(2):
                tok = PE.op(lambda e: e.transpose(ps[:, t * 128:(t + 1) * 128], mpad[:, t, :], ident[:, :]), pw + T["max", b], sig=(t == 1))
                pw = []
            T["mT", b] = tok
            v = VE.op(lambda e: e.tensor_copy(mpt[:, 0, :], ps[0:16, 0:256]), tok + W("mrow", b - 1))
            v = VE.op(lambda e: e.tensor_tensor(mT[:, 0, :], ps[0:16, 0:256], mpt[:, 0, :], ALU.subtract), v)
            release(bs, v)
            v = VE.op(lambda e: e.tensor_copy(mpt[:, 1, :], mT[:, 0, :]), v)
            v = VE.op(lambda e: e.tensor_tensor(mpt[:, 2, :], mT[:, 0, :], mpt[:, 1, :], ALU.subtract), v)
            T["mrow", b] = dma([(s[96 + p:97 + p, 0, :, :], mpt[:, p, :]) for p in range(3)], v)

        def c_exp(h):
            def run(b):
                s = st_[b % 2]
                bs, ps, pw = ering.take()
                for k in range(2):
                    tok = PE.op(lambda e: e.matmul(ps[:, k * 256:(k + 1) * 256], s[0:99, 1, h, k * 128:(k + 1) * 128], s[0:99, 0, h, :],
                                                   start=True, stop=True), pw + T["mrow", b] + T["stack", b], sig=(k == 1))
                    pw = []
                sl = (H * b + h) % 6
                T["ST", b] = tok
                a = AC.op(lambda e: e.activation(PT[:, sl, :, :].rearrange("p b n -> p (b n)"), ps, ACT.Exp, scale=0.25),
                          tok + T.get(("PTfree", sl), end1))
                release(bs, a)
                T["PTexp", sl] = a
            return run

        obank = {}

        def c_PV(hg):
            def run(b):
                if hg % 2 == 0:
                    obank[0] = oring.take()
                obs, o, ow = obank[0]
                c = (hg % 2) * 256
                for k in range(2):
                    for j in range(4):
                        h = 4 * hg + j
                        sl = (H * b + h) % 6
                        tok = PE.op(lambda e: e.matmul(o[32 * j:32 * j + 32, c:c + 256], vv[b % 3][:, k, h, :], PT[:, sl, k, :],
                                                       start=(k == 0), stop=(k == 1)), T["PTexp", sl] + (ow if hg % 2 == 0 else []) + T["vv", b],
                                    sig=(j == 3 and k == 1))
                for j in range(4):
                    T["PTfree", (H * b + 4 * hg + j) % 6] = tok
                if hg % 2 == 1:
                    a = AC.op(lambda e: e.activation(OT[:, hg - 1:hg + 1, :].rearrange("p a n -> p (a n)"), o, ACT.Copy), tok + W("OTt", b - 1))
                    release(obs, a)
                    T["OT", b] = a
                T["PV", b] = tok
            return run

        def c_out(b):
            for t in range(2):
                bs, ps, pw = gring.take()
                for hg in range(4):
                    tok = PE.op(lambda e: e.transpose(ps[:, hg * 128:(hg + 1) * 128], OT[:, hg, t * 128:(t + 1) * 128], ident[:, :]),
                                pw + T["OT", b], sig=(hg == 3))
                    pw = []
                pv = ps.rearrange("p (h d) -> p h d", d=32)
                v = VE.op(lambda e: e.reciprocal(rd[:, t, :].rearrange("p (h d) -> p h d", d=1), pv[:, :, 16:17]), tok)
                v = VE.op(lambda e: e.tensor_tensor(On[:, t, :].rearrange("p (h d) -> p h d", d=16), pv[:, :, 0:16],
                          rd[:, t, :].rearrange("p (h d) -> p h d", d=1).broadcast_to([128, H, 16]), ALU.mult), v + W("Ont", b - 1))
                release(bs, v)
            T["OTt", b] = tok
            T["On", b] = v

        def c_outT(b):
            bs, ps, tok = transpose4(On, T["On", b])
            T["Ont", b] = tok
            T["oT", b] = split(bs, ps, tok, *oT, W("wo", b - 1), bias=vec[:, VEC["wv"]:VEC["wv"] + 2])

        def c_wo(b):
            bs, ps, tok = proj_N("wo", oT, T["oT", b])
            T["wo", b] = tok
            xb = xall[:, b, :, :]
            v = PO.op(lambda e: e.tensor_tensor(xb, xb, bo[:, :].rearrange("p (a n) -> p a n", a=1).broadcast_to([128, 2, 256]), ALU.add),
                      T["xnC", b] + c_tbo)
            xf = xb.rearrange("p a n -> p (a n)")
            v = VE.op(lambda e: e.scalar_tensor_tensor(out=xf, in0=ps, scalar=tg[:, 1:2], in1=xf, op0=ALU.mult, op1=ALU.add), tok + v)
            release(bs, v)
            T["x3", b] = v
            ln_stats("D", b, v)

        def d_apply(b):
            ln_apply("D", b)

        def d_norm(b):
            ln_T("D", b, *x4, W("fc", b - 1) + endA)

        def d_route(b):
            router_mm("D", b, 1, x4)

        def d_top(b):
            m, o = router_top("D", b, 2)
            v = VE.op(lambda e: e.tensor_tensor(rsm[:, :, 0], mx8[:, :, 0], mx8[:, :, 1], ALU.subtract), m)
            a = AC.op(lambda e: e.activation(rsm[:, :, 1], rsm[:, :, 0], ACT.Tanh, scale=0.5), v)
            v = VE.op(lambda e: e.tensor_scalar(rsm[:, :, 2], rsm[:, :, 1], htg[:, 3:4], htg[:, 3:4], ALU.mult, ALU.add), a)
            v2 = VE.op(lambda e: e.tensor_scalar(rsm[:, :, 3], rsm[:, :, 2], -1.0, tg[:, 3:4], ALU.mult, ALU.add), v)
            v = VE.op(lambda e: e.tensor_tensor(oh1[:, :, :], oh1[:, :, :], rsm[:, :, 2:3].broadcast_to([128, 2, 8]), ALU.mult), v + o)
            v2 = VE.op(lambda e: e.tensor_tensor(oh2[:, :, :], oh2[:, :, :], rsm[:, :, 3:4].broadcast_to([128, 2, 8]), ALU.mult), v2 + o)
            T["gatD", b] = VE.op(lambda e: e.tensor_tensor(gat[:, b % 2, :, :], oh1[:, :, :], oh2[:, :, :], ALU.add), v + v2 + W("x4", b - 2))

        def d_up(i):
            def run(b):
                bs, ps, pw = G[0].take()
                pw = pw + T["xTD", b] + wtok[f"f{i}"]
                for j in range(2):
                    for k in range(2):
                        tok = mm3(ps[:, j * 256:(j + 1) * 256], hl(base[f"f{i}"], lambda m: m[:, k * 256 + j * 128:k * 256 + j * 128 + 128]),
                                  hl(x4, lambda a: a[:, k, :]), k == 0, k == 1, pw, sig=(j == 1 and k == 1))
                        pw = []
                T["fc", b] = tok
                n = 4 * b + i
                h32 = stage[:, n % 4, :]
                a = AC.op(lambda e: e.activation(h32, ps, ACT.Gelu), tok + (W("h32", n - 4) if n > 3 else stage_free[n % 4]))
                release(bs, a)
                T["gelu", n] = a
            return run

        def d_split(i):
            def run(b):
                n = 4 * b + i
                a = T["gelu", n]
                h32 = stage[:, n % 4, :]
                c = VE.op(lambda e: e.tensor_copy(hh[:, i, :], h32), a + (W("pj", n - 4) if n > 3 else endA))
                Q = PO if i % 2 else VE
                T["h32", n] = Q.op(lambda e: e.tensor_tensor(hlo[:, i, :], h32, hh[:, i, :].bitcast(F32), ALU.subtract), a + c)
            return run

        wait_end = []

        def d_down(x_):
            i, j = x_ // 2, x_ % 2

            def run(b):
                n = 4 * b + i
                if x_ == 0:
                    acc[b] = [T["gatD", b] + T["x3", b]] * 2
                bs, ps, pw = G[0].take()
                pw = pw + T["h32", n] + wtok[f"p{i}"]
                for t in range(2):
                    tok = mm3(ps[:, t * 256:(t + 1) * 256], hl((hh, hlo), lambda m: m[:, i, j * 256 + t * 128:j * 256 + t * 128 + 128]),
                              hl(base[f"p{i}"], lambda m: m[:, j * 256:(j + 1) * 256]), True, True, pw, sig=(t == 1))
                    pw = []
                T["pj", n] = tok
                weigh(b, bs, ps, tok, x_)
                if x_ == 7:
                    T["x4", b] = acc[b][0] + acc[b][1]
                    wait_end.extend(dma([(out_d[b], xall[:, b, :, :])], T["x4", b]))
            return run

        c_load(0)
        c_load(1)
        slots = [(3, c_out), (4, d_up(0)), (4, d_split(0)), (0, c_qk), (4, d_up(1)), (4, d_split(1)), (3, c_outT), (0, c_v), (4, d_up(2)), (4, d_split(2)),
                 (3, c_wo), (4, d_up(3)), (4, d_split(3)), (0, c_rope(0))]
        extra = {1: [(0, c_rope(1))], 2: [(3, d_apply)], 3: [(3, d_norm)], 5: [(-1, c_stats)], 6: [(3, d_route)], 7: [(0, c_parts), (-1, c_apply)],
                 9: [(3, d_top)], 11: [(-1, c_norm)]}
        for h in range(H):
            slots += [(1, c_max(h)), (2, c_exp(h))]
            slots += extra.get(h, [])
            if h % 2 == 1:
                slots.append((4, d_down(h // 2)))
            if h % 4 == 0 and h:
                slots.append((2, c_PV(h // 4 - 1)))
        slots += [(1, c_maxT), (2, c_PV(3)), (0, c_stack)]
        pipeline(slots, -1, NB + 4)

        for s, v in wait_end:
            nc.sync.wait_ge(s, v)


def tables():
    inv = 1.0 / 10000.0 ** (np.arange(0, 16, 2, dtype=np.float32) / np.float32(16))
    f = np.arange(S, dtype=np.float32)[:, None] * inv[None, :].astype(np.float32)
    emb = np.concatenate([f, f], -1).astype(np.float32)
    cos, sin = np.cos(emb).T, np.sin(emb).T
    sin = np.concatenate([-sin[:8], sin[8:]], 0)
    rope = np.stack([np.repeat(cos, 8, 0), np.repeat(sin, 8, 0)], 1).astype(np.float32)
    iota = np.tile(np.arange(8, dtype=np.float32), (128, 1))
    return np.ascontiguousarray(rope), iota, np.eye(128, dtype=np.float32)


def kernel(**inputs):
    import concourse.bacc as _bacc
    from concourse.bass_utils import run_bass_kernel_spmd as _run

    a = {k: np.asarray(v) for k, v in inputs.items()}

    def heads(w):
        return w.reshape((8, 2, 16) + w.shape[1:]).swapaxes(0, 1).swapaxes(1, 2).reshape(w.shape)

    for n in ("Wq", "bq", "Wk", "bk"):
        a["L1_xattn_" + n] = heads(a["L1_xattn_" + n])

    def km(w):
        return w.T.reshape(-1, 128, w.shape[0]).transpose(1, 0, 2)

    mats = [km(a[n]).reshape(128, 512) for n in ["L0_xattn_Wq_c", "L0_xattn_Wk_c", "L0_xattn_Wq_s", "L0_xattn_Wk_s",
                                                 "L0_xattn_Wv_s", "L0_xattn_Wv_c"]]
    g = km(a["L0_xattn_Wg"])
    mats += [g[:, 0:2].reshape(128, 512), g[:, 2:4].reshape(128, 512)]
    mats += [km(a["L0_ffn_expert_w"][i]).reshape(128, 512) for i in range(8)]
    r = np.zeros((128, 2, 2, 128), np.float32)
    r[:, 0, :, 0:8] = km(a["L0_ffn_router_w"])
    r[:, 1, :, 0:8] = km(a["L1_ffn_w_gate"])
    mats += [r.reshape(128, 512)]
    mats += [km(a[n]).reshape(128, 512) for n in ["L1_xattn_Wq", "L1_xattn_Wk", "L1_xattn_Wv", "L1_xattn_Wo"]]
    fc = a["L1_ffn_w_fc"].reshape(4, 256, 256)
    mats += [km(fc[i]).reshape(128, 512) for i in range(4)]
    pj = a["L1_ffn_w_proj"].transpose(2, 0, 1).reshape(128, 4, 512)
    mats += [pj[:, i] for i in range(4)]
    vec = np.zeros((128, 22), np.float32)
    for i, n in enumerate(["L0_xattn_bq_c", "L0_xattn_bk_c", "L0_xattn_bq_s", "L0_xattn_bk_s", "L0_xattn_bv_s", "L0_xattn_bv_c",
                           "L0_xattn_bg", "L1_xattn_bq", "L1_xattn_bk", "L1_xattn_bv"]):
        vec[:, 2 * i:2 * i + 2] = a[n].reshape(2, 128).T
    vec[0:8, 20] = a["L0_ffn_router_b"]
    eb = np.zeros((128, 256), np.float32)
    eb[0:8] = a["L0_ffn_expert_b"]
    gg = np.tile(np.concatenate([a["g_xattn"], a["g_ffn"]]), (128, 1))
    rope, iota, ident = tables()
    arrays = {
        "x_d": a["x"].reshape(8, 2, 128, 256).transpose(0, 2, 1, 3),
        "ctx_d": a["ctx_1024"].transpose(0, 2, 1).reshape(8, 2, 128, 256).transpose(0, 2, 1, 3).reshape(8, 128, 512),
        "mats_d": np.stack(mats, 1), "vec_d": vec, "bo_d": np.tile(a["L1_xattn_bo"], (128, 1)), "g_d": gg, "eb_d": eb,
        "rope_d": rope, "iota_d": iota, "id_d": ident,
    }
    arrays = {k: np.ascontiguousarray(v) for k, v in arrays.items()}
    nc = _bacc.Bacc("TRN2", target_bir_lowering=False, num_devices=1)
    args = [nc.dram_tensor(k, v.shape, F32, kind="ExternalInput").ap() for k, v in arrays.items()]
    args.append(nc.dram_tensor("out_d", (8, 128, 2, 256), F32, kind="ExternalOutput").ap())
    flamingo(nc, *args)
    res = _run(nc, [arrays], core_ids=[0])
    return res.results[0]["out_d"].reshape(8, 128, 2, 256).transpose(0, 2, 1, 3).reshape(8, 256, 256)
```

```python
from contextlib import ExitStack

import numpy as np

import concourse.bass as bass
from concourse import mybir

F32 = mybir.dt.float32
F32R = mybir.dt.float32r
BF16 = mybir.dt.bfloat16
U32 = mybir.dt.uint32
ALU = mybir.AluOpType
ACT = mybir.ActivationFunctionType
AX = mybir.AxisListType.X

NB = 8
S = 256
D = 256
E = 8
H = 16
EPS = 1e-5

MATS = ["qc", "kc", "qs", "ks", "vs", "vc", "g0", "g1"] + [f"e{i}" for i in range(8)] + \
       ["r"] + ["wq", "wk", "wv", "wo"] + [f"f{i}" for i in range(4)] + [f"p{i}" for i in range(4)]
MI = {n: i for i, n in enumerate(MATS)}
VEC = {n: 2 * i for i, n in enumerate(["qc", "kc", "qs", "ks", "vs", "vc", "g", "wq", "wk", "wv", "rb"])}


class Queue:

    def __init__(self, eng, sem, serial=False):
        self.eng, self.sem, self.n, self.seen, self.serial = eng, sem, 0, {}, serial

    def op(self, fn, waits=(), sig=True):
        if self.serial and self.n:
            waits = list(waits) + [(self.sem, self.n)]
        need = {}
        for sem, v in waits:
            if v > self.seen.get(id(sem), 0):
                self.seen[id(sem)] = v
                need[id(sem)] = (sem, v)
        for sem, v in need.values():
            self.eng.wait_ge(sem, v)
        i = fn(self.eng)
        if not sig:
            return []
        i.then_inc(self.sem, 1)
        self.n += 1
        return [(self.sem, self.n)]


def flamingo(nc, x_d, ctx_d, mats_d, vec_d, bo_d, g_d, eb_d, rope_d, iota_d, id_d, out_d):
    with ExitStack() as st:
        def sb(name, shape, dt=F32):
            return st.enter_context(nc.sbuf_tensor(name, shape, dt))

        nsem = [0]

        def sem():
            nsem[0] += 1
            return st.enter_context(nc.semaphore(f"s{nsem[0]}"))

        PE, AC, VE, SP = (Queue(e, sem()) for e in (nc.tensor, nc.scalar, nc.vector, nc.sync))
        PO = Queue(nc.gpsimd, sem(), serial=True)

        def dma(parts, waits=(), q=None):
            q = q or SP
            s = sem()
            for i, (o, a) in enumerate(parts):
                q.op(lambda e, o=o, a=a: e.dma_start(o, a).then_inc(s, 16), waits if i == 0 else (), sig=False)
            return [(s, 16 * len(parts))]

        T = {}

        def W(name, b):
            return T[name, b] if b >= 0 else []

        xall = sb("xall", [128, NB, 2, 256])
        vec = sb("vec", [128, 22])
        gb = sb("gb", [128, 4])
        tg = sb("tg", [128, 4])
        htg = sb("htg", [128, 4])
        hbg = sb("hbg", [128, 2])
        bo = sb("bo", [128, 256])
        rope = sb("rope", [128, 2, 256])
        iota = sb("iota", [128, 8])
        ident = sb("ident", [128, 128])
        nhalf = sb("nhalf", [128, 2])
        stage = sb("stage", [128, 4, 512])
        wr_h = sb("wr_h", [128, 512], F32R)
        wr_l = sb("wr_l", [128, 512], F32R)
        wA = [sb(f"wA{i}", [128, 8, 512], F32R) for i in range(2)]
        wB = [sb(f"wB{i}", [128, 8, 512], F32R) for i in range(2)]
        base = {}
        for i, n in enumerate(MATS):
            if n == "r":
                base[n] = (wr_h[:, :], wr_l[:, :])
            else:
                j = i if i < 16 else i - 17
                reg = wA if (i < 8 or 17 <= i < 21) else wB
                k = i if i < 8 else (i - 8 if i < 16 else (i - 17 if i < 21 else i - 21))
                base[n] = (reg[0][:, k, :], reg[1][:, k, :])
        xn = sb("xn", [128, 2, 2, 256])
        stt = sb("stt", [128, 2, 2, 6])
        mv = sb("mv", [128, 2, 2, 2])
        ve = sb("ve", [128, 2])
        rstd = sb("rstd", [128, 2, 2])
        xh = sb("xh", [128, 2, 256], F32R)
        xl = sb("xl", [128, 2, 256], F32R)
        lt = sb("lt", [128, 256])
        lg = sb("lg", [128, 2, 8])
        mx8 = sb("mx8", [128, 2, 8])
        ix8 = sb("ix8", [128, 2, 8], U32)
        ixf = sb("ixf", [128, 2, 8])
        oh1 = sb("oh1", [128, 2, 8])
        oh2 = sb("oh2", [128, 2, 8])
        rex = sb("rex", [128, 2, 8])
        rsm = sb("rsm", [128, 2, 4])
        gat = sb("gat", [128, 2, 2, 8])
        cx = sb("cx", [128, 2, 512])
        ch = sb("ch", [128, 2, 256], F32R)
        cl = sb("cl", [128, 2, 256], F32R)
        psum = st.enter_context(nc.psum_tensor("psum", [128, 8, 512], F32))
        bank_free = [[] for _ in range(8)]

        class Ring:
            def __init__(self, banks, width=1):
                self.banks, self.width, self.at = banks, width, 0

            def take(self):
                k = (self.at * self.width) % len(self.banks)
                self.at += 1
                bs = self.banks[k:k + self.width]
                waits = [t for b in bs for t in bank_free[b]]
                for b in bs:
                    bank_free[b] = None
                return bs, psum[:, bs[0]:bs[0] + self.width, :].rearrange("p a n -> p (a n)"), waits

        def release(bs, toks):
            for b in bs:
                bank_free[b] = list(toks)

        def hl(pair, f):
            return f(pair[0]), f(pair[1])

        def mm3(out, lhs, rhs, start, stop, waits=(), sig=False):
            seq = [(lhs[0], rhs[0]), (lhs[0], rhs[1]), (lhs[1], rhs[0])]
            tok = []
            for i, (a, m) in enumerate(seq):
                last = i == 2
                tok = PE.op(lambda e, a=a, m=m, i=i, last=last: e.matmul(out, a, m, start=start and i == 0, stop=stop and last),
                            waits if i == 0 else (), sig=sig and last)
            return tok

        ph1 = ExitStack()
        x2k = (sb("x2h1", [128, 2, 256], F32R), sb("x2l1", [128, 2, 256], F32R))

        def s1(name, shape, dt=F32):
            return ph1.enter_context(nc.sbuf_tensor(name, shape, dt))

        pr = {n: (s1(n + "h", [128, 2, 256], F32R), s1(n + "l", [128, 2, 256], F32R)) for n in ["qc", "kc", "qs", "ks", "vs", "vc"]}
        P1 = [s1(f"P1{i}", [128, 2, 256]) for i in range(2)]
        PT1 = [(s1(f"PT{i}h", [128, 2, 256], F32R), s1(f"PT{i}l", [128, 2, 256], F32R)) for i in range(2)]
        sm = [s1(f"sm{i}", [128, 8]) for i in range(2)]
        cf = [s1(f"cf{i}", [128, 2, 256]) for i in range(2)]
        cs = [(s1(f"cs{i}h", [128, 2, 256], F32R), s1(f"cs{i}l", [128, 2, 256], F32R)) for i in range(2)]
        gt = s1("gt", [128, 2, 256])
        dd = s1("dd", [128, 2, 256])
        uu = s1("uu", [128, 2, 256])
        mxn = s1("mxn", [128, 2, 256])
        x2 = [(s1("x2h0", [128, 2, 256], F32R), s1("x2l0", [128, 2, 256], F32R)), x2k]
        C, X = (ch, cl), (xh, xl)
        ebh = s1("ebh", [128, 256], F32R)
        ebl = s1("ebl", [128, 256], F32R)
        gpad = s1("gpad", [128, 2, 128])
        gTh = s1("gTh", [128, 256], F32R)
        gTl = s1("gTl", [128, 256], F32R)

        c_vec = dma([(vec[:, :], vec_d)])
        c_id = dma([(ident[:, :], id_d)])
        c_g = dma([(gb[:, :], g_d)])
        def load_ctx(name, b, waits):
            T["cx", name, b] = dma([(cx[:, b % 2, :], ctx_d[b])], waits)

        PO.op(lambda e: e.memset(nhalf[:, :], -0.5))
        c_nh = PO.op(lambda e: e.memset(gpad[:, :, :], 0.0))
        c_tg = AC.op(lambda e: e.activation(tg[:, :], gb[:, :], ACT.Tanh), c_g)
        c_hbg = VE.op(lambda e: e.tensor_scalar(hbg[:, :], vec[:, VEC["g"]:VEC["g"] + 2], 0.5, None, ALU.mult), c_vec)

        for b in range(2):
            load_ctx("A", b, ())
            T["x", b] = dma([(xall[:, b, :, :], x_d[b])])
        stage_free = [[] for _ in range(4)]
        wtok = {}
        nst = [0]

        def load_mat(n):
            k = nst[0] % 4
            nst[0] += 1
            T["stage", n] = k, dma([(stage[:, k, :], mats_d[:, MI[n], :])], stage_free[k])
            stage_free[k] = None

        def split_mat(n, waits=(), Q=None):
            k, t = T["stage", n]
            h, l = base[n]
            a = AC.op(lambda e: e.activation(h, stage[:, k, :], ACT.Copy), t + list(waits))
            v = (Q or VE).op(lambda e: e.tensor_tensor(l, stage[:, k, :], h.bitcast(F32), ALU.subtract), a + t)
            stage_free[k] = v
            wtok[n] = v

        mv_free, xn_free = [[], []], [[], []]
        ring = Ring(list(range(8)))
        G = [ring]
        rt_free = {"lt": []}

        def ln_stats(name, b, x_tok):
            i = "ABCD".index(name) % 2
            s = []
            for t in range(2):
                s += VE.op(lambda e: e.bn_stats(stt[:, i, t, :], xall[:, b, t, :]), x_tok)
            a = []
            for t in range(2):
                a += VE.op(lambda e: e.bn_aggr(mv[:, i, t, :], stt[:, i, t, :]), s + mv_free[i])
            p = PO.op(lambda e: e.tensor_scalar(ve[:, :], mv[:, i, :, 1], EPS, None, ALU.add), a + c_nh)
            T["rstd" + name, b] = a + PO.op(lambda e: e.tensor_tensor(rstd[:, i, :], ve[:, :], nhalf[:, :], ALU.pow), p + mv_free[i])

        def ln_apply(name, b):
            i = "ABCD".index(name) % 2
            n = []
            for t in range(2):
                n += VE.op(lambda e: e.tensor_scalar(xn[:, i, t, :], xall[:, b, t, :], mv[:, i, t, 0:1],
                                                     rstd[:, i, t:t + 1], ALU.subtract, ALU.mult), T["rstd" + name, b] + xn_free[i])
            mv_free[i] = n
            T["xn" + name, b] = n

        def ln_T(name, b, h, l, used):
            i = "ABCD".index(name) % 2
            bs, ps, tok = transpose4(xn[:, i, :, :], T["xn" + name, b])
            xn_free[i] = tok
            T["xT" + name, b] = split(bs, ps, tok, h, l, used)

        def transpose4(src, toks):
            bs, ps, w = G[0].take()
            for k in range(2):
                for t in range(2):
                    tok = PE.op(lambda e, k=k, t=t: e.transpose(ps[:, k * 256 + t * 128:k * 256 + t * 128 + 128],
                                                               src[:, t, k * 128:(k + 1) * 128], ident[:, :]),
                                w + list(toks) + c_id, sig=(k == 1 and t == 1))
                    w = []
            return bs, ps, tok

        def split(bs, ps, tok, h, l, free, bias=None):
            hf, lf = h.rearrange("p a n -> p (a n)"), l.rearrange("p a n -> p (a n)")
            if bias is None:
                a = AC.op(lambda e: e.activation(hf, ps, ACT.Copy), tok + list(free))
                v = VE.op(lambda e: e.tensor_tensor(lf, ps, hf.bitcast(F32), ALU.subtract), a)
            else:
                for k in range(2):
                    a = AC.op(lambda e, k=k: e.activation(h[:, k, :], ps[:, k * 256:(k + 1) * 256], ACT.Identity,
                                                          bias=bias[:, k:k + 1]), tok + list(free) + c_vec)
                for k in range(2):
                    v = VE.op(lambda e, k=k: e.scalar_tensor_tensor(
                        out=l[:, k, :], in0=ps[:, k * 256:(k + 1) * 256], scalar=bias[:, k:k + 1],
                        in1=h[:, k, :].bitcast(F32), op0=ALU.add, op1=ALU.subtract), a)
            release(bs, v)
            return v

        def proj_T(w, act, waits):
            bs, ps, pw = G[0].take()
            pw = pw + list(waits) + wtok[w]
            for o in range(2):
                for k in range(2):
                    tok = mm3(ps[:, o * 256:(o + 1) * 256], hl(base[w], lambda m: m[:, k * 256 + o * 128:k * 256 + o * 128 + 128]),
                              hl(act, lambda a: a[:, k, :]), k == 0, k == 1, pw, sig=(o == 1 and k == 1))
                    pw = []
            return bs, ps, tok

        def proj_N(w, act, waits):
            bs, ps, pw = G[0].take()
            pw = pw + list(waits) + wtok[w]
            for t in range(2):
                for k in range(2):
                    tok = mm3(ps[:, t * 256:(t + 1) * 256], hl(act, lambda a: a[:, k, t * 128:(t + 1) * 128]),
                              hl(base[w], lambda m: m[:, k * 256:(k + 1) * 256]), k == 0, k == 1, pw, sig=(t == 1 and k == 1))
                    pw = []
            return bs, ps, tok

        def router_mm(name, b, half, act):
            bs, ps, pw = G[0].take()
            pw = pw + T["xT" + name, b] + wtok["r"]
            for k in range(2):
                tok = mm3(ps[:, 0:256], hl(base["r"], lambda m: m[:, half * 256 + k * 128:half * 256 + k * 128 + 128]),
                          hl(act, lambda a: a[:, k, :]), k == 0, k == 1, pw, sig=(k == 1))
                pw = []
            if half == 0:
                a = AC.op(lambda e: e.activation(lt[0:8, :], ps[0:8, 0:256], ACT.Identity, bias=vec[0:8, VEC["rb"]:VEC["rb"] + 1]),
                          tok + rt_free["lt"])
            else:
                a = AC.op(lambda e: e.activation(lt[0:8, :], ps[0:8, 0:256], ACT.Copy), tok + rt_free["lt"])
            release(bs, a)
            T["lt" + name, b] = a

        def router_top(name, b, n):
            bs, ps, pw = G[0].take()
            pw = pw + T["lt" + name, b]
            for t in range(2):
                tok = PE.op(lambda e: e.transpose(ps[:, t * 8:t * 8 + 8], lt[0:8, t * 128:(t + 1) * 128], ident[0:8, 0:8]),
                            pw, sig=(t == 1))
                pw = []
            rt_free["lt"] = tok
            v = VE.op(lambda e: e.tensor_copy(lg[:, :, :].rearrange("p a n -> p (a n)"), ps[:, 0:16]), tok)
            release(bs, v)
            m, i = [], []
            for t in range(2):
                m += VE.op(lambda e: e.max(mx8[:, t, :], lg[:, t, :]), v)
            for t in range(2):
                i += VE.op(lambda e: e.max_index(ix8[:, t, :], mx8[:, t, :], lg[:, t, :]), m)
            f = VE.op(lambda e: e.tensor_copy(ixf[:, :, :], ix8[:, :, :]), i + T["iota", 0])
            o = []
            for t in range(2):
                for oh, c in ((oh1, 0), (oh2, 1))[:n]:
                    o += VE.op(lambda e: e.tensor_scalar(oh[:, t, :], iota[:, :], ixf[:, t, c:c + 1], None, ALU.is_equal), f)
            return m, o

        def a_load(b):
            if b < NB:
                load_ctx("A", b, W("ctxsplitA", b - 2))
                T["x", b] = dma([(xall[:, b, :, :], x_d[b])])

        def ctx_split(name, b, free):
            cf_ = cx[:, b % 2, :]
            a = AC.op(lambda e: e.activation(ch[:, :, :].rearrange("p a n -> p (a n)"), cf_, ACT.Copy), T["cx", name, b] + free)
            T["ctxsplit" + name, b] = (VE if b < 2 else PO).op(lambda e: e.tensor_tensor(cl[:, :, :].rearrange("p a n -> p (a n)"), cf_,
                                            ch[:, :, :].rearrange("p a n -> p (a n)").bitcast(F32), ALU.subtract), a + free)

        def a_stats(b):
            ln_stats("A", b, T["x", b])

        def a_apply(b):
            ln_apply("A", b)

        def a_norm(b):
            f = W("projA", b - 1)
            ln_T("A", b, xh, xl, f)
            ctx_split("A", b, f)
            a_load(b + 2)

        def a_proj(*names):
            def run(b):
                for n in names:
                    act, tr = {"qc": (X, 1), "ks": (C, 1), "qs": (C, 1), "kc": (X, 1), "vs": (C, 0), "vc": (X, 0)}[n]
                    bs, ps, tok = (proj_T if tr else proj_N)(n, act, T["xTA", b] + T["ctxsplitA", b])
                    free = W({"qc": "S0", "ks": "S0", "qs": "S1", "kc": "S1", "vs": "PV0", "vc": "PV1"}[n], b - 1)
                    T[n, b] = split(bs, ps, tok, *pr[n], free, bias=vec[:, VEC[n]:VEC[n] + 2] if tr else None)
                    T["projA", b] = tok
            return run

        def a_scores(i):
            q, k = [("qc", "ks"), ("qs", "kc")][i]
            s = sm[i]

            def run(b):
                bs, ps, pw = G[0].take()
                pw = pw + T[q, b] + T[k, b]
                for t in range(2):
                    for kk in range(2):
                        tok = mm3(ps[:, t * 256:(t + 1) * 256], hl(pr[q], lambda m: m[:, kk, t * 128:(t + 1) * 128]),
                                  hl(pr[k], lambda m: m[:, kk, :]), kk == 0, kk == 1, pw, sig=(t == 1 and kk == 1))
                        pw = []
                T[f"S{i}", b] = tok
                v = VE.op(lambda e: e.tensor_reduce(s[:, 0:2], ps.rearrange("p (a n) -> p a n", a=2), AX, ALU.max, negate=True), tok + W(f"P{i}", b - 1))
                v = VE.op(lambda e: e.tensor_scalar(s[:, 2:4], s[:, 0:2], 1.0 / 16, None, ALU.mult), v)
                for t in range(2):
                    a = AC.op(lambda e: e.activation(P1[i][:, t, :], ps[:, t * 256:(t + 1) * 256], ACT.Exp, bias=s[:, 2 + t:3 + t],
                                                     scale=1.0 / 16, accum_out=s[:, 4 + t:5 + t]), v + W(f"PTt{i}", b - 1))
                release(bs, a)
                T[f"E{i}", b] = a
            return run

        def a_scale(i):
            s = sm[i]

            def run(b):
                v = VE.op(lambda e: e.reciprocal(s[:, 6:8], s[:, 4:6]), T[f"E{i}", b])
                r = []
                for t in range(2):
                    r += VE.op(lambda e: e.tensor_scalar(P1[i][:, t, :], P1[i][:, t, :], s[:, 6 + t:7 + t], None, ALU.mult), v)
                T[f"P{i}", b] = r
            return run

        def a_PT(i):
            def run(b):
                bs, ps, tok = transpose4(P1[i], T[f"P{i}", b])
                T[f"PTt{i}", b] = tok
                T[f"PT{i}", b] = split(bs, ps, tok, *PT1[i], W(f"PV{i}", b - 1))
            return run

        def a_PV(i):
            v_ = ["vs", "vc"][i]

            def run(b):
                bs, ps, pw = G[0].take()
                pw = pw + T[f"PT{i}", b] + T[v_, b]
                for o in range(2):
                    for k in range(2):
                        tok = mm3(ps[:, o * 256:(o + 1) * 256], hl(pr[v_], lambda m: m[:, k, o * 128:(o + 1) * 128]),
                                  hl(PT1[i], lambda m: m[:, k, :]), k == 0, k == 1, pw, sig=(o == 1 and k == 1))
                        pw = []
                T[f"PV{i}", b] = tok
                bias = vec[:, VEC[v_]:VEC[v_] + 2]
                for k in range(2):
                    a = AC.op(lambda e: e.activation(cf[i][:, k, :], ps[:, k * 256:(k + 1) * 256], ACT.Identity, bias=bias[:, k:k + 1]),
                              tok + W("uu", b - 1))
                release(bs, a)
                v = VE.op(lambda e: e.tensor_copy(cs[i][0][:, :, :], cf[i][:, :, :]), a + W("gate", b - 1))
                T[f"cs{i}", b] = PO.op(lambda e: e.tensor_tensor(cs[i][1][:, :, :], cf[i][:, :, :], cs[i][0][:, :, :].bitcast(F32), ALU.subtract), v)
            return run

        def a_gate(b):
            bs, ps, pw = G[0].take()
            pw = pw + T["cs0", b] + T["cs1", b] + wtok["g0"] + wtok["g1"]
            for o in range(2):
                for k in range(4):
                    tok = mm3(ps[:, o * 256:(o + 1) * 256], hl(base[f"g{k // 2}"], lambda m: m[:, (k % 2) * 256 + o * 128:(k % 2) * 256 + o * 128 + 128]),
                              hl(cs[k // 2], lambda m: m[:, k % 2, :]), k == 0, k == 3, pw, sig=(o == 1 and k == 3))
                    pw = []
            T["gate", b] = tok
            p = PO.op(lambda e: e.tensor_tensor(dd[:, :, :], cf[0][:, :, :], cf[1][:, :, :], ALU.subtract), T["cs0", b] + T["cs1", b] + W("uu", b - 1))
            v1 = PO.op(lambda e: e.tensor_tensor(uu[:, :, :], cf[0][:, :, :], cf[1][:, :, :], ALU.add), p + W("mixT", b - 1))
            for k in range(2):
                a = AC.op(lambda e: e.activation(gt[:, k, :], ps[:, k * 256:(k + 1) * 256], ACT.Tanh, bias=hbg[:, k:k + 1], scale=0.5),
                          tok + c_hbg + W("uu", b - 1))
            release(bs, a)
            v = VE.op(lambda e: e.tensor_tensor(dd[:, :, :], dd[:, :, :], gt[:, :, :], ALU.mult), a + p)
            T["uu", b] = VE.op(lambda e: e.tensor_tensor(uu[:, :, :], uu[:, :, :], dd[:, :, :], ALU.add), v + v1)

        def a_mix(b):
            bs, ps, pw = G[0].take()
            pw = pw + T["uu", b]
            for t in range(2):
                for k in range(2):
                    tok = PE.op(lambda e: e.transpose(ps[:, t * 256 + k * 128:t * 256 + k * 128 + 128], uu[:, k, t * 128:(t + 1) * 128],
                                                      ident[:, :]), pw, sig=(t == 1 and k == 1))
                    pw = []
            T["mixT", b] = tok
            xb = xall[:, b, :, :].rearrange("p a n -> p (a n)")
            v = VE.op(lambda e: e.scalar_tensor_tensor(out=xb, in0=ps, scalar=htg[:, 0:1], in1=xb, op0=ALU.mult, op1=ALU.add), tok + c_htg)
            release(bs, v)
            T["x1", b] = v
            ln_stats("B", b, v)

        def b_apply(b):
            ln_apply("B", b)

        def b_norm(b):
            ln_T("B", b, *x2[b % 2], W("exp", b - 2))

        def b_route(b):
            router_mm("B", b, 0, x2[b % 2])

        def b_top(b):
            m, o = router_top("B", b, 1)
            v = VE.op(lambda e: e.tensor_tensor(rex[:, :, :], lg[:, :, :], mx8[:, :, 0:1].broadcast_to([128, 2, 8]), ALU.subtract), m)
            a = AC.op(lambda e: e.activation(rex[:, :, :], rex[:, :, :], ACT.Exp), v)
            v = VE.op(lambda e: e.reduce_sum(rsm[:, :, 0], rex[:, :, :], axis=AX), a)
            v = VE.op(lambda e: e.reciprocal(rsm[:, :, 1], rsm[:, :, 0]), v)
            v = VE.op(lambda e: e.tensor_scalar(rsm[:, :, 2], rsm[:, :, 1], tg[:, 2:3], None, ALU.mult), v + c_tg)
            v = VE.op(lambda e: e.tensor_tensor(gat[:, b % 2, :, :], oh1[:, :, :], rsm[:, :, 2:3].broadcast_to([128, 2, 8]), ALU.mult), v + o + W("x2", b - 2))
            T["gat", b] = v
            acc[b] = [T["gat", b] + T["x1", b]] * 2
            T["gpad", b] = VE.op(lambda e: e.tensor_copy(gpad[:, :, 0:8], gat[:, b % 2, :, :]), v + W("gTt", b - 1) + c_nh)

        def b_gT(b):
            bs, ps, pw = G[0].take()
            for t in range(2):
                tok = PE.op(lambda e: e.transpose(ps[:, t * 128:(t + 1) * 128], gpad[:, t, :], ident[:, :]), pw + T["gpad", b], sig=(t == 1))
                pw = []
            T["gTt", b] = tok
            a = AC.op(lambda e: e.activation(gTh[:, :], ps[:, 0:256], ACT.Copy), tok + W("bias", b - 1))
            v = VE.op(lambda e: e.tensor_tensor(gTl[:, :], ps[:, 0:256], gTh[:, :].bitcast(F32), ALU.subtract), a)
            release(bs, v)
            T["gT", b] = v

        def b_bias(b):
            bs, ps, pw = G[0].take()
            pw = pw + T["gT", b] + T["eb", 0]
            for t in range(2):
                tok = mm3(ps[:, t * 256:(t + 1) * 256], hl((gTh, gTl), lambda m: m[:, t * 128:(t + 1) * 128]), (ebh[:, :], ebl[:, :]), True, True, pw, sig=(t == 1))
                pw = []
            T["bias", b] = tok
            xb = xall[:, b, :, :].rearrange("p a n -> p (a n)")
            v = VE.op(lambda e: e.tensor_tensor(xb, ps, xb, ALU.add), tok + acc[b][0] + acc[b][1])
            release(bs, v)
            acc[b] = [v, v]

        acc = {}

        def weigh(b, bs, ps, tok, x_):
            for t in range(2):
                acc[b][t] = VE.op(lambda e: e.scalar_tensor_tensor(
                    out=xall[:, b, t, :], in0=ps[:, t * 256:(t + 1) * 256], scalar=gat[:, b % 2, t, x_:x_ + 1],
                    in1=xall[:, b, t, :], op0=ALU.mult, op1=ALU.add), tok + acc[b][t])
            release(bs, acc[b][0] + acc[b][1])

        def b_expert(x_):
            def run(b):
                bs, ps, tok = proj_N(f"e{x_}", x2[b % 2], T["xTB", b])
                weigh(b, bs, ps, tok, x_)
                T["exp", b] = tok
                T["x2", b] = acc[b][0] + acc[b][1]
            return run

        ph1.close()
        qp = sb("qp", [128, 2, 2, 256])
        qr = sb("qr", [128, 2, 2, 256])
        parts = sb("parts", [128, 2, 3, 2, 256], BF16)
        vv = [sb(f"vv{i}", [128, 2, H, 32]) for i in range(3)]
        st_ = [sb(f"st{i}", [99, 2, H, 256], BF16) for i in range(2)]
        mpad = sb("mpad", [128, 2, 128])
        mT = sb("mT", [16, 256])
        mpt = sb("mpt", [16, 3, 256], BF16)
        PT = sb("PT", [128, 6, 2, 256])
        x4 = (sb("x4h", [128, 2, 256], F32R), sb("x4l", [128, 2, 256], F32R))
        OT = sb("OT", [128, 4, 256])
        rd = sb("rd", [128, 2, H])
        On = sb("On", [128, 2, 256])
        oT = (sb("oTh", [128, 2, 256], F32R), sb("oTl", [128, 2, 256], F32R))
        hh, hlo = wA[0][:, 4:8, :], wA[1][:, 4:8, :]

        g2, oring, mring, ering = Ring([0, 1, 2]), Ring([3]), Ring([4, 5]), Ring([6, 7])

        def c_load(b):
            if b < NB:
                load_ctx("C", b, W("ctxsplitC", b - 2) if b > 1 else T["ctxsplitA", NB - 1])

        def c_stats(b):
            ln_stats("C", b, T["x2", b])

        def c_apply(b):
            ln_apply("C", b)

        def c_norm(b):
            f = W("projC", b - 1) if b else T["projA", NB - 1]
            ln_T("C", b, xh, xl, f)
            ctx_split("C", b, f)
            c_load(b + 2)

        def c_qk(b):
            for i, (n, act) in enumerate([("wq", X), ("wk", C)]):
                bs, ps, tok = proj_T(n, act, T["xTC", b] + T["ctxsplitC", b])
                for k in range(2):
                    a = AC.op(lambda e: e.activation(qp[:, i, k, :], ps[:, k * 256:(k + 1) * 256], ACT.Identity,
                              bias=vec[:, VEC[n] + k:VEC[n] + k + 1]), tok + W("rope", b - 1) + end_p())
                release(bs, a)
            src = qp[:, :, :, :].rearrange("p i k n -> p (i k n)")
            dst = qr[:, :, :, :].rearrange("p i k n -> p (i k n)")
            T["qp", b] = a
            T["qr", b] = dma([(dst[64 * w:64 * w + 64, :], src[64 - 64 * w:128 - 64 * w, :]) for w in range(2)], a + W("rope", b - 1))

        def c_v(b):
            bs, ps, tok = proj_N("wv", C, [])
            T["projC", b] = tok
            a = AC.op(lambda e: e.activation(vv[b % 3][:, :, :, 0:16], ps.rearrange("p (t h d) -> p t h d", t=2, d=16), ACT.Copy),
                      tok + W("PV", b - 3) + T["clear", "vv"])
            release(bs, a)
            T["vv", b] = a

        def copy(Q, out, src, waits):
            if Q is AC:
                return AC.op(lambda e: e.activation(out, src, ACT.Copy), waits)
            return Q.op(lambda e: e.tensor_copy(out, src), waits)

        def c_rope(i):
            def run(b):
                w = T["qp", b] + T["qr", b] + T["iota", 0]
                a = (VE if b < 1 else PO).op(lambda e: e.tensor_tensor(qp[:, i, :, :], qp[:, i, :, :], rope[:, 0:1, :].broadcast_to([128, 2, 256]), ALU.mult), w)
                c = VE.op(lambda e: e.tensor_tensor(qr[:, i, :, :], qr[:, i, :, :], rope[:, 1:2, :].broadcast_to([128, 2, 256]), ALU.mult), w)
                a = (VE if b < 1 else PO).op(lambda e: e.tensor_tensor(qp[:, i, :, :], qp[:, i, :, :], qr[:, i, :, :], ALU.add), a + c)
                T["turn", i, b] = a
                c = AC.op(lambda e: e.activation(parts[:, i, 0, :, :], qp[:, i, :, :], ACT.Copy), a + W("stack", b - 1))
                a = PO.op(lambda e: e.tensor_tensor(qp[:, i, :, :], qp[:, i, :, :], parts[:, i, 0, :, :], ALU.subtract), a + c)
                T["part", i, b] = a
            return run

        def c_parts(b):
            r = []
            for i in range(2):
                a = T["part", i, b]
                c = AC.op(lambda e: e.activation(parts[:, i, 1, :, :], qp[:, i, :, :], ACT.Copy), a)
                r += (VE if b < 1 else PO).op(lambda e: e.tensor_tensor(parts[:, i, 2, :, :], qp[:, i, :, :], parts[:, i, 1, :, :], ALU.subtract), c + a)
            T["rope", b] = r

        def c_stack(b):
            moves = []
            for i, order in enumerate([(0, 0, 0, 1, 1, 2), (0, 1, 2, 0, 1, 0)]):
                for c, p in enumerate(order):
                    moves.append((st_[b % 2][16 * c:16 * c + 16, i, :, :],
                                  parts[:, i, p, :, :].rearrange("p o n -> p (o n)")))
            T["stack", b] = dma(moves, T["rope", b] + W("ST", b - 2) + W("mT", b - 2) + T["clear", "st", b % 2])

        def c_max(h):
            def run(b):
                s = st_[b % 2]
                bs, ps, pw = mring.take()
                for t in range(2):
                    tok = PE.op(lambda e: e.matmul(ps[:, t * 256:(t + 1) * 256], s[0:96, 0, h, t * 128:(t + 1) * 128], s[0:96, 1, h, :],
                                                   start=True, stop=True), pw + T["stack", b], sig=(t == 1))
                    pw = []
                v = VE.op(lambda e: e.tensor_reduce(mpad[:, :, h:h + 1], ps.rearrange("p (a n) -> p a n", a=2), AX, ALU.max, negate=True),
                          tok + W("mT", b - 1) + T["clear", "mpad"])
                release(bs, v)
                T["max", h, b] = v
            return run

        def c_maxT(b):
            s = st_[b % 2]
            bs, ps, pw = G[0].take()
            pw = pw + [t for h in range(H) for t in T["max", h, b]]
            for t in range(2):
                tok = PE.op(lambda e: e.transpose(ps[:, t * 128:(t + 1) * 128], mpad[:, t, :], ident[:, :]), pw, sig=(t == 1))
                pw = []
            T["mT", b] = tok
            v = VE.op(lambda e: e.tensor_copy(mpt[:, 0, :], ps[0:16, 0:256]), tok + W("mrow", b - 1))
            v = VE.op(lambda e: e.tensor_tensor(mT[:, :], ps[0:16, 0:256], mpt[:, 0, :], ALU.subtract), v)
            release(bs, v)
            v = VE.op(lambda e: e.tensor_copy(mpt[:, 1, :], mT[:, :]), v)
            v = VE.op(lambda e: e.tensor_tensor(mpt[:, 2, :], mT[:, :], mpt[:, 1, :], ALU.subtract), v)
            T["mrow", b] = dma([(s[96 + p:97 + p, 0, :, :], mpt[:, p, :]) for p in range(3)], v)

        def c_exp(h):
            def run(b):
                s = st_[b % 2]
                bs, ps, pw = ering.take()
                for k in range(2):
                    tok = PE.op(lambda e: e.matmul(ps[:, k * 256:(k + 1) * 256], s[0:99, 1, h, k * 128:(k + 1) * 128], s[0:99, 0, h, :],
                                                   start=True, stop=True), pw + T["mrow", b] + T["stack", b], sig=(k == 1))
                    pw = []
                sl = (H * b + h) % 6
                T["ST", b] = tok
                a = AC.op(lambda e: e.activation(PT[:, sl, :, :].rearrange("p b n -> p (b n)"), ps, ACT.Exp, scale=0.25),
                          tok + T.get(("PTfree", sl), end_1()))
                release(bs, a)
                T["PTexp", sl] = a
            return run

        obank = {}

        def c_PV(hg):
            def run(b):
                if hg % 2 == 0:
                    obank[0] = oring.take()
                obs, o, ow = obank[0]
                c = (hg % 2) * 256
                for k in range(2):
                    for j in range(4):
                        h = 4 * hg + j
                        sl = (H * b + h) % 6
                        tok = PE.op(lambda e: e.matmul(o[32 * j:32 * j + 32, c:c + 256], vv[b % 3][:, k, h, :], PT[:, sl, k, :],
                                                       start=(k == 0), stop=(k == 1)), T["PTexp", sl] + (ow if hg % 2 == 0 else []) + T["vv", b],
                                    sig=(j == 3 and k == 1))
                for j in range(4):
                    T["PTfree", (H * b + 4 * hg + j) % 6] = tok
                if hg % 2 == 1:
                    a = AC.op(lambda e: e.activation(OT[:, hg - 1:hg + 1, :].rearrange("p a n -> p (a n)"), o, ACT.Copy), tok + W("OTt", b - 1))
                    release(obs, a)
                    T["OT", b] = a
                T["PV", b] = tok
            return run

        def c_out(b):
            for t in range(2):
                bs, ps, pw = G[0].take()
                for hg in range(4):
                    tok = PE.op(lambda e: e.transpose(ps[:, hg * 128:(hg + 1) * 128], OT[:, hg, t * 128:(t + 1) * 128], ident[:, :]),
                                pw + T["OT", b], sig=(hg == 3))
                    pw = []
                pv = ps.rearrange("p (h d) -> p h d", d=32)
                v = VE.op(lambda e: e.reciprocal(rd[:, t, :].rearrange("p (h d) -> p h d", d=1), pv[:, :, 16:17]), tok)
                v = VE.op(lambda e: e.tensor_tensor(On[:, t, :].rearrange("p (h d) -> p h d", d=16), pv[:, :, 0:16],
                          rd[:, t, :].rearrange("p (h d) -> p h d", d=1).broadcast_to([128, H, 16]), ALU.mult), v + W("Ont", b - 1))
                release(bs, v)
            T["OTt", b] = tok
            T["On", b] = v

        def c_outT(b):
            bs, ps, tok = transpose4(On, T["On", b])
            T["Ont", b] = tok
            T["oT", b] = split(bs, ps, tok, *oT, W("wo", b - 1), bias=vec[:, VEC["wv"]:VEC["wv"] + 2])

        def c_wo(b):
            bs, ps, tok = proj_N("wo", oT, T["oT", b])
            T["wo", b] = tok
            xb = xall[:, b, :, :]
            v = VE.op(lambda e: e.tensor_tensor(xb, xb, bo[:, :].rearrange("p (a n) -> p a n", a=1).broadcast_to([128, 2, 256]), ALU.add),
                      T["xnC", b] + T["bo", 0])
            xf = xb.rearrange("p a n -> p (a n)")
            v = VE.op(lambda e: e.scalar_tensor_tensor(out=xf, in0=ps, scalar=tg[:, 1:2], in1=xf, op0=ALU.mult, op1=ALU.add), tok + v)
            release(bs, v)
            T["x3", b] = v
            ln_stats("D", b, v)

        def d_apply(b):
            ln_apply("D", b)

        def d_norm(b):
            ln_T("D", b, *x4, W("fc", b - 1) + end_a())

        def d_route(b):
            router_mm("D", b, 1, x4)

        def d_top(b):
            m, o = router_top("D", b, 2)
            v = VE.op(lambda e: e.tensor_tensor(rsm[:, :, 0], mx8[:, :, 0], mx8[:, :, 1], ALU.subtract), m)
            a = AC.op(lambda e: e.activation(rsm[:, :, 1], rsm[:, :, 0], ACT.Tanh, scale=0.5), v)
            v = VE.op(lambda e: e.tensor_scalar(rsm[:, :, 2], rsm[:, :, 1], htg[:, 3:4], htg[:, 3:4], ALU.mult, ALU.add), a)
            v2 = VE.op(lambda e: e.tensor_scalar(rsm[:, :, 3], rsm[:, :, 2], -1.0, tg[:, 3:4], ALU.mult, ALU.add), v)
            v = VE.op(lambda e: e.tensor_tensor(oh1[:, :, :], oh1[:, :, :], rsm[:, :, 2:3].broadcast_to([128, 2, 8]), ALU.mult), v + o)
            v2 = VE.op(lambda e: e.tensor_tensor(oh2[:, :, :], oh2[:, :, :], rsm[:, :, 3:4].broadcast_to([128, 2, 8]), ALU.mult), v2 + o)
            T["gatD", b] = VE.op(lambda e: e.tensor_tensor(gat[:, b % 2, :, :], oh1[:, :, :], oh2[:, :, :], ALU.add), v + v2 + W("x4", b - 2))

        def d_up(i):
            def run(b):
                bs, ps, pw = G[0].take()
                pw = pw + T["xTD", b] + wtok[f"f{i}"]
                for j in range(2):
                    for k in range(2):
                        tok = mm3(ps[:, j * 256:(j + 1) * 256], hl(base[f"f{i}"], lambda m: m[:, k * 256 + j * 128:k * 256 + j * 128 + 128]),
                                  hl(x4, lambda a: a[:, k, :]), k == 0, k == 1, pw, sig=(j == 1 and k == 1))
                        pw = []
                T["fc", b] = tok
                n = 4 * b + i
                h32 = stage[:, n % 4, :]
                a = AC.op(lambda e: e.activation(h32, ps, ACT.Gelu), tok + (W("h32", n - 4) + weighed(n - 4) if n > 3 else stage_free[n % 4]))
                release(bs, a)
                T["gelu", n] = a
            return run

        def d_split(i):
            def run(b):
                n = 4 * b + i
                a = T["gelu", n]
                h32 = stage[:, n % 4, :]
                c = copy((AC, VE, VE, VE)[i], hh[:, i, :], h32, a + (W("pj", n - 4) if n > 3 else end_a()))
                T["h32", n] = (PO, PO, VE, PO)[i].op(lambda e: e.tensor_tensor(hlo[:, i, :], h32, hh[:, i, :].bitcast(F32), ALU.subtract), a + c)
            return run

        wait_end = []
        acc_gate = {}

        def weigh_2(b, bs, ps, tok, x_, n):
            for t in range(2):
                y = stage[:, n % 4, t * 256:(t + 1) * 256]
                a = AC.op(lambda e: e.activation(y, ps[:, t * 256:(t + 1) * 256], ACT.Copy, scale=gat[:, b % 2, t, x_:x_ + 1]),
                          tok + acc_gate[b] + T.get(("weighed", n, t), []))
                acc[b][t] = PO.op(lambda e: e.tensor_tensor(xall[:, b, t, :], xall[:, b, t, :], y, ALU.add), a + acc[b][t])
                T["weighed", n, t] = acc[b][t]
            release(bs, a)

        def weighed(n):
            return T.get(("weighed", n, 0), []) + T.get(("weighed", n, 1), [])

        def d_down(x_):
            i, j = x_ // 2, x_ % 2

            def run(b):
                n = 4 * b + i
                if x_ == 0:
                    acc[b] = [T["gatD", b] + T["x3", b]] * 2
                    acc_gate[b] = T["gatD", b]
                bs, ps, pw = G[0].take()
                pw = pw + T["h32", n] + wtok[f"p{i}"]
                for t in range(2):
                    tok = mm3(ps[:, t * 256:(t + 1) * 256], hl((hh, hlo), lambda m: m[:, i, j * 256 + t * 128:j * 256 + t * 128 + 128]),
                              hl(base[f"p{i}"], lambda m: m[:, j * 256:(j + 1) * 256]), True, True, pw, sig=(t == 1))
                    pw = []
                T["pj", n] = tok
                if x_ in (3,):
                    weigh_2(b, bs, ps, tok, x_, n)
                else:
                    weigh(b, bs, ps, tok, x_)
                if x_ == 7:
                    T["x4", b] = acc[b][0] + acc[b][1]
                    wait_end.extend(dma([(out_d[b], xall[:, b, :, :])], T["x4", b]))
            return run

        last = NB - 1

        def end_a():
            return T["projA", last] + T["gate", last] + T["PV1", last]

        def end_p():
            return T["S1", last] + T["PV1", last]

        def end_q():
            return end_p() + T["gate", last] + T["mixT", last] + T["uu", last] + T["cs0", last] + T["cs1", last]

        def end_1():
            return end_q() + T["exp", last - 1] + T["bias", last] + T["gTt", last] + T["gT", last]

        def mats(*names, after=lambda: [], load=True, cut=True, Q=None):
            def run(k):
                for n in names:
                    if load:
                        load_mat(n)
                    if cut:
                        split_mat(n, after(), Q)
            return run

        def small(k):
            i = nst[0] % 4
            nst[0] += 1
            t = dma([(iota[:, :], iota_d), (stage[:, i, 0:256], eb_d), (bo[:, :], bo_d), (rope[:, :, :], rope_d)], stage_free[i])
            a = AC.op(lambda e: e.activation(ebh[:, :], stage[:, i, 0:256], ACT.Copy), t)
            T["eb", 0] = stage_free[i] = VE.op(lambda e: e.tensor_tensor(ebl[:, :], stage[:, i, 0:256], ebh[:, :].bitcast(F32), ALU.subtract), a)
            T["bo", 0] = VE.op(lambda e: e.tensor_scalar(bo[:, :], bo[:, :], tg[:, 1:2], None, ALU.mult), t + c_tg)
            T["iota", 0] = t

        def clear_p(k):
            for i in range(3):
                t = VE.op(lambda e: e.memset(vv[i][:, :, :, 16:32], 0.0), end_p())
            for i in range(3):
                t = VE.op(lambda e: e.memset(vv[i][:, :, :, 16:17], 1.0), t)
            T["clear", "vv"] = t

        def clear_q(k):
            T["clear", "st", 0] = PO.op(lambda e: e.memset(st_[0][96:99, 1, :, :], 1.0), end_q())

        def clear_1(k):
            T["clear", "st", 1] = VE.op(lambda e: e.memset(st_[1][96:99, 1, :, :], 1.0), end_1())
            T["clear", "mpad"] = PO.op(lambda e: e.memset(mpad[:, :, :], 0.0), end_1())

        def pipeline(slots, first, last, late=None):
            for k in range(first, last):
                for slot in slots:
                    if slot[0] == "at":
                        if slot[1] == k:
                            slot[2](k)
                        continue
                    lag, fn = slot
                    if 0 <= k - lag < NB and (lag, k) != late:
                        fn(k - lag)

        def at(k, fn):
            return "at", k, fn

        c_htg = VE.op(lambda e: e.tensor_scalar(htg[:, :], tg[:, :], 0.5, None, ALU.mult), c_tg)
        x_ = b_expert

        def ld(*n):
            return mats(*n, cut=False)

        def sp(*n, after=lambda: [], Q=None):
            return mats(*n, load=False, after=after, Q=Q)

        end_w = lambda: T["projA", last]
        pipeline([
            at(9, lambda k: c_qk(0)), (1, a_PV(0)), (2, x_(1)), (1, a_PV(1)), at(8, clear_p), (2, x_(0)), at(0, sp("ks", Q=PO)),
            (2, b_gT), at(9, lambda k: b_gT(last)), at(8, lambda k: c_load(1)), at(8, lambda k: c_stats(0)), (-1, a_stats),
            at(8, lambda k: c_load(0)), at(0, ld("vs")), at(-1, ld("qc", "ks", "qs", "kc")), (2, x_(2)),
            at(8, sp("wq", "wk", after=end_w)), (-1, a_apply), (0, a_proj("qc")), at(8, lambda k: c_apply(0)), at(0, sp("qs")),
            (2, b_bias), (1, a_gate), at(9, lambda k: b_bias(last)), at(0, ld("vc")), at(9, lambda k: c_stats(1)), (0, a_proj("ks")),
            (2, x_(3)), (1, a_mix), at(8, clear_q), at(9, lambda k: c_v(0)), at(0, sp("kc", Q=PO)), at(0, ld("g0")), (0, a_proj("qs")),
            (0, a_scores(0)), at(9, lambda k: c_rope(0)(0)), at(0, ld("g1")), at(8, ld("wv", "wo")), (1, b_apply), (0, a_proj("kc")),
            (2, x_(4)), at(8, lambda k: c_norm(0)), at(9, lambda k: c_apply(1)), at(0, sp("vs")), at(9, lambda k: c_rope(1)(0)),
            (1, b_norm), at(0, sp("g1", Q=PO)), (0, a_proj("vs")), (2, x_(5)), at(0, sp("vc")), at(9, lambda k: x_(0)(last)),
            (0, a_scores(1)), at(0, ld("r")), at(0, sp("g0", Q=PO)), (0, a_scale(0)), at(9, lambda k: c_norm(1)), (1, b_route),
            at(9, lambda k: c_parts(0)), (0, a_scale(1)), at(1, mats("e4", "e5", "e6", "e7")), at(1, ld("e0", "e1", "e2", "e3")),
            at(8, sp("wv", "wo", after=end_w)), (0, a_proj("vc")), (2, x_(6)), (0, a_PT(0)), at(0, sp("r", Q=PO)), at(0, small),
            (0, a_PT(1)), (-1, a_norm), at(7, ld("wq", "wk")), at(-1, sp("qc")), at(1, sp("e0", "e1", "e2", "e3")), (1, b_top),
            (2, x_(7)),
        ], -1, NB + 2, late=(2, NB + 1))
        c_stack(0)
        clear_1(0)
        G[0] = g2
        end_e = lambda: T["exp", last]
        pipeline([
            (4, d_up(0)), (3, c_out), (2, c_maxT), (4, d_split(0)), (4, d_up(1)), (4, d_split(1)), (3, c_outT),
            at(1, lambda k: x_(1)(last)), (0, c_qk), (3, c_wo), at(2, ld("f0", "f1")), at(1, lambda k: x_(4)(last)), (4, d_up(2)),
            (4, d_up(3)), (2, c_exp(0)), (4, d_split(2)), (2, c_exp(1)), (1, c_max(1)), (0, c_v), (0, c_rope(0)), (1, c_max(2)),
            (3, d_apply), (1, c_max(0)), at(2, sp("f0", "f1", after=end_e)), (4, d_down(0)), (4, d_split(3)), (2, c_exp(2)),
            (1, c_max(5)), (3, d_norm), (2, c_exp(3)), (4, d_down(1)), at(2, ld("f2", "f3")), (2, c_exp(4)), (0, c_rope(1)),
            (1, c_max(4)), (-1, c_stats), at(1, lambda k: x_(6)(last)), (1, c_max(3)), (2, c_PV(0)), (2, c_exp(5)), (4, d_down(2)),
            (2, c_exp(6)), (3, d_route), at(2, sp("f2", "f3", after=end_e, Q=PO)), (1, c_max(7)), at(2, ld("p0", "p1")),
            at(1, lambda k: x_(5)(last)), (1, c_max(6)), (2, c_exp(7)), (4, d_down(3)), (1, c_max(8)), (1, c_max(9)), (-1, c_apply),
            (2, c_exp(9)), (2, c_exp(8)), (0, c_parts), (3, d_top), (2, c_PV(1)), (1, c_max(10)), at(1, lambda k: x_(2)(last)),
            (4, d_down(4)), (2, c_exp(11)), at(2, ld("p2", "p3")), (2, c_exp(10)), (1, c_max(11)), (-1, c_norm), (4, d_down(5)),
            at(1, lambda k: x_(7)(last)), (2, c_exp(12)), (2, c_PV(2)), (2, c_exp(13)), (1, c_max(13)), (2, c_exp(14)), (4, d_down(6)),
            (2, c_exp(15)), at(2, sp("p0", "p1", after=end_e)), (0, c_stack), (1, c_max(14)), (4, d_down(7)),
            at(1, lambda k: x_(3)(last)), (1, c_max(12)), (2, c_PV(3)), at(2, sp("p2", "p3", after=end_e, Q=PO)), (1, c_max(15)),
        ], 1, NB + 4)

        for s, v in wait_end:
            nc.sync.wait_ge(s, v)


def tables():
    inv = 1.0 / 10000.0 ** (np.arange(0, 16, 2, dtype=np.float32) / np.float32(16))
    f = np.arange(S, dtype=np.float32)[:, None] * inv[None, :].astype(np.float32)
    emb = np.concatenate([f, f], -1).astype(np.float32)
    cos, sin = np.cos(emb).T, np.sin(emb).T
    sin = np.concatenate([-sin[:8], sin[8:]], 0)
    rope = np.stack([np.repeat(cos, 8, 0), np.repeat(sin, 8, 0)], 1).astype(np.float32)
    iota = np.tile(np.arange(8, dtype=np.float32), (128, 1))
    return np.ascontiguousarray(rope), iota, np.eye(128, dtype=np.float32)


def kernel(**inputs):
    import concourse.bacc as _bacc
    from concourse.bass_utils import run_bass_kernel_spmd as _run

    a = {k: np.asarray(v) for k, v in inputs.items()}

    def heads(w):
        return w.reshape((8, 2, 16) + w.shape[1:]).swapaxes(0, 1).swapaxes(1, 2).reshape(w.shape)

    for n in ("Wq", "bq", "Wk", "bk"):
        a["L1_xattn_" + n] = heads(a["L1_xattn_" + n])

    def km(w):
        return w.T.reshape(-1, 128, w.shape[0]).transpose(1, 0, 2)

    mats = [km(a[n]).reshape(128, 512) for n in ["L0_xattn_Wq_c", "L0_xattn_Wk_c", "L0_xattn_Wq_s", "L0_xattn_Wk_s",
                                                 "L0_xattn_Wv_s", "L0_xattn_Wv_c"]]
    g = km(a["L0_xattn_Wg"])
    mats += [g[:, 0:2].reshape(128, 512), g[:, 2:4].reshape(128, 512)]
    mats += [km(a["L0_ffn_expert_w"][i]).reshape(128, 512) for i in range(8)]
    r = np.zeros((128, 2, 2, 128), np.float32)
    r[:, 0, :, 0:8] = km(a["L0_ffn_router_w"])
    r[:, 1, :, 0:8] = km(a["L1_ffn_w_gate"])
    mats += [r.reshape(128, 512)]
    mats += [km(a[n]).reshape(128, 512) for n in ["L1_xattn_Wq", "L1_xattn_Wk", "L1_xattn_Wv", "L1_xattn_Wo"]]
    fc = a["L1_ffn_w_fc"].reshape(4, 256, 256)
    mats += [km(fc[i]).reshape(128, 512) for i in range(4)]
    pj = a["L1_ffn_w_proj"].transpose(2, 0, 1).reshape(128, 4, 512)
    mats += [pj[:, i] for i in range(4)]
    vec = np.zeros((128, 22), np.float32)
    for i, n in enumerate(["L0_xattn_bq_c", "L0_xattn_bk_c", "L0_xattn_bq_s", "L0_xattn_bk_s", "L0_xattn_bv_s", "L0_xattn_bv_c",
                           "L0_xattn_bg", "L1_xattn_bq", "L1_xattn_bk", "L1_xattn_bv"]):
        vec[:, 2 * i:2 * i + 2] = a[n].reshape(2, 128).T
    vec[0:8, 20] = a["L0_ffn_router_b"]
    eb = np.zeros((128, 256), np.float32)
    eb[0:8] = a["L0_ffn_expert_b"]
    gg = np.tile(np.concatenate([a["g_xattn"], a["g_ffn"]]), (128, 1))
    rope, iota, ident = tables()
    arrays = {
        "x_d": a["x"].reshape(8, 2, 128, 256).transpose(0, 2, 1, 3),
        "ctx_d": a["ctx_1024"].transpose(0, 2, 1).reshape(8, 2, 128, 256).transpose(0, 2, 1, 3).reshape(8, 128, 512),
        "mats_d": np.stack(mats, 1), "vec_d": vec, "bo_d": np.tile(a["L1_xattn_bo"], (128, 1)), "g_d": gg, "eb_d": eb,
        "rope_d": rope, "iota_d": iota, "id_d": ident,
    }
    arrays = {k: np.ascontiguousarray(v) for k, v in arrays.items()}
    nc = _bacc.Bacc("TRN2", target_bir_lowering=False, num_devices=1)
    args = [nc.dram_tensor(k, v.shape, F32, kind="ExternalInput").ap() for k, v in arrays.items()]
    args.append(nc.dram_tensor("out_d", (8, 128, 2, 256), F32, kind="ExternalOutput").ap())
    flamingo(nc, *args)
    res = _run(nc, [arrays], core_ids=[0])
    return res.results[0]["out_d"].reshape(8, 128, 2, 256).transpose(0, 2, 1, 3).reshape(8, 256, 256)
```
